# Optimizing a Trainium2 kernel written in Bass

```python
import numpy as np
import jax
import jax.numpy as jnp

def _softmax(x, axis=-1):
    return jax.nn.softmax(x, axis=axis)

def _gelu(x):
    return jax.nn.gelu(x, approximate=True)

def _silu(x):
    return jax.nn.silu(x)

def _sigmoid(x):
    return jax.nn.sigmoid(x)

def _layernorm(x, axis=-1, eps=1e-05):
    m = jnp.mean(x, axis=axis, keepdims=True)
    v = jnp.var(x, axis=axis, keepdims=True)
    return (x - m) / jnp.sqrt(v + eps)

def _scatter_add(tgt, idx, src, axis=0):
    return tgt.at[idx].add(src)

def _segment_sum(src, seg, n):
    return jax.ops.segment_sum(src, seg, n)
kernel_name = 'mk_gnn_resnorm_d1_gnn_r8_a1ea8f'

def setup_inputs(seed: int=0):
    np.random.seed(seed)
    _w = jnp.asarray

    def _rec_inputs():
        import jax
        import jax.numpy as jnp
        _gk = jax.random.key(seed)
        x = -0.0003713 + 1 * jax.random.normal(jax.random.fold_in(_gk, 1), (6250, 256), jnp.float32)
        src = jax.random.randint(jax.random.fold_in(_gk, 2), (100000,), 0, 6250, jnp.int32)
        dst = jnp.minimum((6250 * jax.random.uniform(jax.random.fold_in(_gk, 3), (100000,)) ** 2.0).astype(jnp.int32), 49999)
        _o = jnp.argsort(dst, stable=True)
        src = src[_o]
        dst = dst[_o]
        return (x, src, dst)
    x, src, dst = _rec_inputs()

    def _L0_gnn_setup():
        import jax, jax.numpy as jnp
        import numpy as np
        N_NODES = 6250
        N_EDGES = 100000
        D_IN = 256
        D_HID = 256
        D_OUT = 256
        key = jax.random.key(seed)
        k_x, k_e, k_w1, k_wm = jax.random.split(key, 4)
        input_matrix = jax.random.normal(k_x, (N_NODES, D_IN), dtype=jnp.float32)
        adjacency_coo_matrix = jax.random.randint(k_e, (2, N_EDGES), 0, N_NODES, dtype=jnp.int32)
        fc_w = jax.random.normal(k_w1, (D_IN, D_HID), dtype=jnp.float32) * (1.0 / np.sqrt(D_IN))
        fc_b = jnp.zeros((D_HID,), dtype=jnp.float32)
        lim = np.sqrt(6.0 / (D_IN + D_HID + D_OUT)).astype(np.float32)
        weights_matrix = jax.random.uniform(k_wm, (D_IN + D_HID, D_OUT), dtype=jnp.float32, minval=-lim, maxval=lim)
        return {'input_matrix': input_matrix, 'adjacency_coo_matrix': adjacency_coo_matrix, 'fc_w': fc_w, 'fc_b': fc_b, 'weights_matrix': weights_matrix}
    _L0_gnn_all = _L0_gnn_setup()
    _L0_gnn_in = {k: v for k, v in _L0_gnn_all.items() if k in ('fc_w', 'fc_b', 'weights_matrix')}
    del _L0_gnn_all
    return {'x': x, 'src': src, 'dst': dst, 'L0_gnn_fc_w': _L0_gnn_in['fc_w'], 'L0_gnn_fc_b': _L0_gnn_in['fc_b'], 'L0_gnn_weights_matrix': _L0_gnn_in['weights_matrix']}

def reference(x, src, dst, L0_gnn_fc_w, L0_gnn_fc_b, L0_gnn_weights_matrix):
    import jax
    import jax.numpy as jnp

    def _L0_gnn_ref(input_matrix, adjacency_coo_matrix, fc_w, fc_b, weights_matrix):
        import jax, jax.numpy as jnp
        import numpy as np
        N_NODES = 6250
        N_EDGES = 100000
        D_IN = 256
        D_HID = 256
        D_OUT = 256
        n_nodes = input_matrix.shape[0]
        edge_src = adjacency_coo_matrix[0]
        edge_trg = adjacency_coo_matrix[1]
        neighbors = input_matrix[edge_trg]
        neighbors_repr = jax.nn.relu(neighbors @ fc_w + fc_b)
        aggregated = jax.ops.segment_max(neighbors_repr, edge_src, num_segments=n_nodes)
        aggregated = jnp.maximum(aggregated, 0.0)
        concat = jnp.concatenate([input_matrix, aggregated], axis=1)
        return concat @ weights_matrix
    edge_index = jnp.stack([src, dst])
    x = _layernorm(x + _L0_gnn_ref(x, edge_index, L0_gnn_fc_w, L0_gnn_fc_b, L0_gnn_weights_matrix), axis=-1)
    return x

_drawn_inputs = setup_inputs


def setup_inputs(seed=0):
    import zlib

    import numpy as np

    out = dict(_drawn_inputs(seed))
    spreads = {'L0_gnn_fc_b': (0.0, 0.1)}
    factors = {}
    for name, (base, spread) in spreads.items():
        noise = np.random.default_rng([zlib.crc32(name.encode()), seed]).standard_normal(out[name].shape)
        drawn = base * np.exp(spread * noise) if base else spread * noise
        out[name] = jnp.asarray(drawn.astype(out[name].dtype))
    for name, factor in factors.items():
        out[name] = (out[name] * factor).astype(out[name].dtype)
    return out
```

```python
from contextlib import ExitStack

import concourse.bass as bass
from concourse import mybir

ALU = mybir.AluOpType
ACT = mybir.ActivationFunctionType
F32 = mybir.dt.float32
BF16 = mybir.dt.bfloat16
I32 = mybir.dt.int32

P = 128
D = 256
DC = D // P
NODES = 6250
NP = 125
NT = NODES // NP
SPREAD = 112
EDGES = 100000
EC = EDGES // NP

LOGW = 10
W = 1 << LOGW
LOGN = LOGW + 7
HALF = W // 2
DST_BITS = 13
MARK = 0x20000000
PAD_KEY = float(2.0 ** 127)
SEG0 = MARK >> DST_BITS
LEAD = 64

ROUNDS = -(-EDGES // P)
HR = 17
BODIES = ROUNDS // (2 * HR)
GATHER_GROUPS = [range(0, 4), range(4, 8), range(8, 12), range(12, HR)]
FIX0 = P * ROUNDS
ZERO_ROW = FIX0 + P
TABLE = ZERO_ROW + 1
ROUNDER = float(3 << 22)

HG = 5
GROUPS = NT // HG
LOOPED = 6
EPS = 1e-5

C_ID, C_TRI, C_IOTA, C_SIGN, C_ROW, C_ONE = 0, P, 2 * P, 3 * P, 3 * P + 8, 4 * P
C_ALL = 5 * P


def build(nc, x, src, dst, fc_w, fc_b, wm, consts, out):
    assert NP * NT == NODES and NP * EC == EDGES and 2 * HR * BODIES == ROUNDS and EC <= W
    ctx = ExitStack()
    with ctx:
        def sb(name, shape, dt):
            return ctx.enter_context(nc.sbuf_tensor(name, shape, dt))

        def ps(name, shape):
            return ctx.enter_context(nc.psum_tensor(name, shape, F32))

        def sem(name):
            return ctx.enter_context(nc.semaphore(name))

        keys_dram = nc.dram_tensor("sorted_keys", [LEAD + P * W], F32).ap()
        h_dram = nc.dram_tensor("h_rows", [NODES, D], F32).ap()
        table = nc.dram_tensor("running_max", [TABLE, D], F32).ap()
        table_rounds = table[0:FIX0, :].rearrange("(p c) f -> p c f", c=ROUNDS)

        base = sb("base", [P, NT, D], F32)
        cst = sb("cst", [P, C_ALL], F32)
        w_cat = sb("w_cat", [P, DC, 2 * D], F32)
        w2 = sb("w2", [P, DC, D], F32)
        bias = sb("bias", [1, D], F32)
        xt = sb("xt", [P, 2, DC, P], F32)
        ring = sb("ring", [P, 2 * HR, D], F32)
        runmax = sb("runmax", [P, 2 * HR, D], F32)
        srt = sb("srt", [P, ROUNDS + 1], F32)
        seg = sb("seg", [P, ROUNDS + 1], I32)
        nbr = sb("nbr", [P, ROUNDS], I32)
        same = sb("same", [P, ROUNDS], F32)
        node_p = sb("node_p", [P, ROUNDS], BF16)
        node_i = sb("node_i", [P, ROUNDS], BF16)
        nbr_now = sb("nbr_now", [P, 2, HR], I32)
        same_now = sb("same_now", [P, 2, HR], F32)
        iota = sb("iota", [P, P], BF16)
        hot_p = sb("hot_p", [P, 2, HR, P], BF16)
        hot_i = sb("hot_i", [P, 2, HR, NT], BF16)
        col = sb("col", [P, 16], F32)
        first_at = sb("first_at", [P, 1], I32)
        node_at = sb("node_at", [P, NT], I32)
        stats = sb("stats", [P, 2, HG, 6], F32)
        mv = sb("mv", [P, 2, HG, 2], F32)
        std = sb("std", [P, 2, HG], F32)
        rstd = sb("rstd", [P, 2, HG], F32)
        shift = sb("shift", [P, 2, HG], F32)
        eps = sb("eps", [P, 1], F32)

        flat = ring[:, :, :].rearrange("p a b -> p (a b)")
        keys = [flat[:, 0:W], flat[:, W:2 * W]]
        signed = flat[:, 2 * W:3 * W]
        upper = flat[:, 3 * W:3 * W + HALF]
        src_in = flat[:, 4 * W:4 * W + EC].bitcast(I32)
        dst_in = flat[:, 5 * W:5 * W + EC].bitcast(I32)
        key_bits = keys[1].bitcast(I32)
        flat_max = runmax[:, :, :].rearrange("p a b -> p (a b)")
        node_f = flat_max[:, 20 * D:20 * D + ROUNDS]
        node_t = flat_max[:, 24 * D:24 * D + ROUNDS]
        xg = [runmax[:, s * HG:(s + 1) * HG, :] for s in range(2)]
        hg = [runmax[:, (2 + s) * HG:(3 + s) * HG, :] for s in range(2)]
        first_rows = ring[:, 20, :]
        fix_rows = ring[:, 21, :]
        carry_t = flat[:, 22 * D:22 * D + 2 * (P + 1)].rearrange("p (c n) -> p c n", c=2)
        w_row = flat[:, 25 * D:25 * D + P]
        w_diag = flat[:, 26 * D:26 * D + P]
        cnt, incl, last, first, e_p, s_p, t_a, t_b = (
            flat[:, 27 * D + n * 64:27 * D + n * 64 + NT] for n in range(8))
        agg = [ring[:, s * HG:(s + 1) * HG, :] for s in range(2)]
        y_buf = [runmax[:, s * HG:(s + 1) * HG, :] for s in range(2)]
        o_buf = [runmax[:, (2 + s) * HG:(3 + s) * HG, :] for s in range(2)]

        tp = ps("tp", [P, W])
        bp = ps("bp", [P, W])
        xt_ps = ps("xt_ps", [P, 2, 512])
        mm_ps = ps("mm_ps", [P, 2, 512])
        cnt_ps = tp[:, 0:NT]
        off_ps = tp[:, HALF:HALF + 1]
        z_ps = bp[:, 0:D]
        wrow_ps = bp[:, HALF:HALF + P]
        carry_ps = xt_ps[:, 0, 0:D]

        ident = cst[:, C_ID:C_ID + P]
        tri = cst[:, C_TRI:C_TRI + P]
        ones = cst[:, C_ONE:C_ONE + P]
        L_FIRST, CONT, WHOLE, CARRY_ON, OFF = range(5)

        s_edges = sem("edges_loaded")
        s_consts = sem("consts_loaded")
        s_weights = sem("weights_loaded")
        s_x = [sem(f"x_loaded_{s}") for s in range(2)]
        s_wcat = sem("w_cat_ready")
        s_xt_t = sem("x_transposed")
        s_xt_c = sem("xt_copied")
        s_mm = sem("h_product_done")
        s_h = sem("h_evacuated")
        s_h_st = [sem(f"h_stored_{s}") for s in range(2)]
        s_sort = sem("sort_steps")
        s_signed = sem("signed_pieces")
        s_tr = sem("sort_transposes")
        s_up = sem("upper_copied")
        s_keys_st = sem("keys_stored")
        s_lead = sem("lead_stored")
        s_srt = sem("sorted_loaded")
        s_dec = sem("decoded")
        s_pre = sem("vector_setup")
        s_staged = sem("halves_staged")
        s_pool = sem("pool_halves")
        s_rows = [[sem(f"rows_{h}_{g}") for g in range(len(GATHER_GROUPS))] for h in range(2)]
        s_acc = sem("rounds_done")
        s_tab = [sem(f"table_stored_{h}") for h in range(2)]
        s_hot = sem("onehots_ready")
        s_hot_free = sem("onehots_free")
        s_cnt = sem("count_steps")
        s_off = sem("offsets_ready")
        s_first = sem("first_rows_loaded")
        s_zt = sem("carry_transposes")
        s_fix = sem("fix_steps")
        s_fix_st = sem("fix_rows_stored")
        s_agg = [sem(f"agg_loaded_{j}") for j in range(2 * HG)]
        s_at = sem("agg_transposed")
        s_at_c = sem("agg_copied")
        s_y = sem("agg_product_done")
        s_sum = sem("y_summed")
        s_stat = sem("statistics_ready")
        s_seen = sem("statistics_seen")
        s_var = sem("variance_ready")
        s_std = sem("deviation_ready")
        s_rstd = sem("rstd_ready")
        s_scale = sem("scales_ready")
        s_norm = sem("groups_normed")
        s_out = [sem(f"out_stored_{s}") for s in range(2)]

        PARTS = (slice(0, SPREAD), slice(SPREAD, NP))
        x_tiles = x.rearrange("(p i) f -> p i f", i=NT)
        h_tiles = h_dram.rearrange("(p i) f -> p i f", i=NT)
        out_tiles = out.rearrange("(p i) f -> p i f", i=NT)

        SETUP = 4
        IN_PART = LOGW * (LOGW + 1) // 2
        level_end = {LOGW: SETUP + IN_PART}
        for k in range(LOGW + 1, LOGN + 1):
            level_end[k] = level_end[k - 1] + k + 1
        SORTED = level_end[LOGN]
        held = {LOGW: IN_PART % 2}
        for k in range(LOGW + 1, LOGN + 1):
            held[k] = (held[k - 1] + k) % 2

        def turned_end(k):
            return level_end[k - 1] + (k - LOGW) + 1

        def turned_held(k):
            return (held[k - 1] + k - LOGW) % 2

        base_flat = base[:, :, :].rearrange("p i f -> p (i f)")
        state = runmax[:, 2 * HR - 1, :]
        zeros_p, zeros_i = hot_p[:, 0, 0, :], hot_i[:, 0, 0, :]
        FIX_DONE = 6
        CNT_DONE = 19
        DECODED = 17

        block = ctx.enter_context(nc.Block())

        @block.sync
        def _(sp):
            sp.dma_start(src_in[0:NP, :], src.rearrange("(p c) -> p c", c=EC)).then_inc(s_edges, 16)
            sp.dma_start(dst_in[0:NP, :], dst.rearrange("(p c) -> p c", c=EC)).then_inc(s_edges, 16)
            sp.dma_start(cst[:, :], consts).then_inc(s_consts, 16)

            def load_x(g):
                for part in PARTS:
                    sp.dma_start(xg[g % 2][part, :, :], x_tiles[part, g * HG:(g + 1) * HG, :]).then_inc(s_x[g % 2], 16)

            load_x(0)
            sp.dma_start(w_cat[:, :, 0:D], fc_w.rearrange("(c p) n -> p c n", c=DC)).then_inc(s_weights, 16)
            sp.dma_start(w_cat[:, :, D:2 * D], wm[0:D, :].rearrange("(c p) n -> p c n", c=DC)).then_inc(s_weights, 16)
            sp.dma_start(w2[:, :, :], wm[D:2 * D, :].rearrange("(c p) n -> p c n", c=DC)).then_inc(s_weights, 16)
            sp.dma_start(bias[:, :], fc_b.rearrange("(a n) -> a n", a=1)).then_inc(s_weights, 16)
            load_x(1)
            sp.wait_ge(s_consts, 16)
            sp.dma_start(keys_dram[LEAD - 1:LEAD].rearrange("(a n) -> a n", a=1),
                         cst[0:1, C_IOTA:C_IOTA + 1]).then_inc(s_lead, 16)
            sp.wait_ge(s_acc, 1)
            for h in range(2):
                sp.dma_start(table[ZERO_ROW:ZERO_ROW + 1, h * P:(h + 1) * P], state[0:1, h * P:(h + 1) * P]).then_inc(s_tab[h], 16)
            for g in range(GROUPS):
                sp.wait_ge(s_h, 2 + HG * (g + 1))
                for part in PARTS:
                    sp.dma_start(h_tiles[part, g * HG:(g + 1) * HG, :], hg[g % 2][part, :, :]).then_inc(s_h_st[g % 2], 16)
                if g + 2 < GROUPS:
                    sp.wait_ge(s_xt_t, HG * (g + 1))
                    load_x(g + 2)
            sp.wait_ge(s_sort, SORTED)
            sp.dma_start(keys_dram[LEAD:LEAD + P * W].rearrange("(p c) -> p c", c=W), keys[held[LOGN]]).then_inc(s_keys_st, 16)
            sp.wait_ge(s_keys_st, 16)
            sp.wait_ge(s_lead, 16)
            chunks = keys_dram[LEAD - 1:LEAD - 1 + P * ROUNDS].rearrange("(p c) -> p c", c=ROUNDS)
            sp.dma_start(srt[:, 0:ROUNDS], chunks).then_inc(s_srt, 16)
            ends = keys_dram[LEAD - 1 + ROUNDS:LEAD - 1 + ROUNDS + P * ROUNDS].rearrange("(p c) -> p c", c=ROUNDS)
            sp.dma_start(srt[:, ROUNDS:ROUNDS + 1], ends[:, 0:1], allow_slow_non_contiguous=True).then_inc(s_srt, 16)
            with sp.Fori(0, BODIES) as i:
                for h in range(2):
                    sp.wait_ge(s_acc, 1 + 2 * HR * i + HR * h + HR)
                    sp.dma_start(table_rounds[:, bass.ds(2 * HR * i + HR * h, HR), :],
                                 runmax[:, h * HR:(h + 1) * HR, :]).then_inc(s_tab[h], 16)
            sp.wait_ge(s_fix, FIX_DONE)
            sp.dma_start(table[FIX0:FIX0 + P, :], fix_rows).then_inc(s_fix_st, 16)

            def store(g, s):
                sp.wait_ge(s_norm, g + 1)
                for part in PARTS:
                    sp.dma_start(out_tiles[part, bass.ds(g * HG, HG), :], o_buf[s][part, :, :]).then_inc(s_out[s], 16)

            with sp.Fori(0, GROUPS // 2) as b:
                for s in range(2):
                    store(2 * b + s, s)
            for s in range(2):
                sp.wait_ge(s_out[s], 32 * (GROUPS // 2))
            for s in range(2):
                sp.wait_ge(s_h_st[s], 32 * (GROUPS // 2))

        @block.gpsimd
        def _(pool):
            pool.wait_ge(s_consts, 16)
            pool.wait_ge(s_weights, 64)
            for c in range(DC):
                diag = w_cat[:, c, D + c * P:D + (c + 1) * P]
                pool.tensor_tensor(diag, diag, ident, ALU.add)
            pool.tensor_copy(iota[:, :], cst[:, C_IOTA:C_IOTA + P])
            pool.memset(eps[:, :], EPS).then_inc(s_wcat, 1)
            for s in range(2):
                pool.wait_ge(s_h_st[s], 32 * (GROUPS // 2))
            with pool.Fori(0, BODIES) as i:
                for h in range(2):
                    pool.wait_ge(s_staged, 2 * i + h + 1)
                    pool.sem_inc(s_pool, 1)
                    for g, rounds in enumerate(GATHER_GROUPS):
                        for r in rounds:
                            pool.indirect_dma_start(
                                ring[:, h * HR + r, :], None, h_dram,
                                bass.IndirectOffsetOnAxis(ap=nbr_now[:, h, r:r + 1], axis=0)).then_inc(s_rows[h][g], 16)
            for h in range(2):
                pool.wait_ge(s_tab[h], 16 + 16 * BODIES)
            pool.indirect_dma_start(first_rows, None, table[0:FIX0, :],
                                    bass.IndirectOffsetOnAxis(ap=first_at[:, :], axis=0)).then_inc(s_first, 16)
            pool.wait_ge(s_cnt, CNT_DONE)
            pool.wait_ge(s_fix_st, 16)
            for t in range(NT):
                if t >= 2 * HG:
                    pool.wait_ge(s_at, t - 2 * HG + 1)
                pool.indirect_dma_start(agg[t // HG % 2][:, t % HG, :], None, table,
                                        bass.IndirectOffsetOnAxis(ap=node_at[:, t:t + 1], axis=0)).then_inc(s_agg[t % (2 * HG)], 16)

        def h_products(pe, g, s):
            def turn(j):
                slot = (s * HG + j) % 2
                if j == 0:
                    pe.wait_ge(s_x[s], 16 * (g - s) + 32)
                pe.wait_ge(s_xt_c, g * HG + j + 1)
                for c in range(DC):
                    ins = pe.transpose(xt_ps[:, slot, c * P:c * P + NP], xg[s][0:NP, j, c * P:(c + 1) * P],
                                       ident[0:NP, 0:NP])
                ins.then_inc(s_xt_t, 1)

            def product(j):
                slot = (s * HG + j) % 2
                pe.wait_ge(s_xt_c, g * HG + j + 3)
                pe.wait_ge(s_h, g * HG + j + 1)
                for c in range(DC):
                    pe.matmul(mm_ps[0:NP, slot, :], xt[:, slot, c, 0:NP], w_cat[:, c, :], start=(c == 0), stop=False,
                              skip_group_check=True)
                pe.matmul(mm_ps[0:NP, slot, 0:D], ones[0:1, 0:NP], bias[0:1, :], start=False, stop=True,
                          skip_group_check=True).then_inc(s_mm, 1)

            turn(0)
            for j in range(HG):
                if j + 1 < HG:
                    turn(j + 1)
                product(j)

        def copy_turned(act, turned, copied, n, slot):
            act.wait_ge(turned, n + 1)
            act.copy(xt[:, slot, :, 0:NP],
                     xt_ps[:, slot, 0:D].rearrange("p (c n) -> p c n", c=DC)[:, :, 0:NP]).then_inc(copied, 1)

        def h_evacuate(act, g, s):
            copy_turned(act, s_xt_t, s_xt_c, g * HG, s * HG % 2)
            for j in range(HG):
                slot = (s * HG + j) % 2
                if j + 1 < HG:
                    copy_turned(act, s_xt_t, s_xt_c, g * HG + j + 1, 1 - slot)
                act.wait_ge(s_mm, g * HG + j + 1)
                if j == 0 and not (isinstance(g, int) and g < 2):
                    act.wait_ge(s_h_st[s], 16 * (g - s))
                act.activation(hg[s][0:NP, j, :], mm_ps[0:NP, slot, 0:D], ACT.Relu)
                act.copy(base_flat[0:NP, bass.ds((g * HG + j) * D, D)], mm_ps[0:NP, slot, D:2 * D]).then_inc(s_h, 1)

        def level_base(k, per_level):
            return per_level * (k - LOGW - 1)

        def pairs(buf, d):
            v = buf.rearrange("p (a two d) -> p a two d", two=2, d=d)
            return v[:, :, 0, :], v[:, :, 1, :]

        @block.tensor
        def _(pe):
            pe.wait_ge(s_wcat, 1)
            for s in range(2):
                h_products(pe, s, s)
            with pe.Fori(1, LOOPED // 2) as b:
                for s in range(2):
                    h_products(pe, 2 * b + s, s)
            for k in range(LOGW + 1, LOGN + 1):
                for b in range(W // P):
                    if b % 2 == 0:
                        pe.wait_ge(s_signed, level_base(k, 4) + b // 2 + 1)
                    ins = pe.transpose(tp[:, b * P:(b + 1) * P], signed[:, b * P:(b + 1) * P], ident)
                    if b % 4 == 3:
                        ins.then_inc(s_tr, 1)
                pe.wait_ge(s_sort, turned_end(k))
                for b in (4, 5, 6, 7, 0, 1, 2, 3):
                    ins = pe.transpose(bp[:, b * P:(b + 1) * P], keys[turned_held(k)][:, b * P:(b + 1) * P], ident)
                    if b % 4 == 3:
                        ins.then_inc(s_tr, 1)
                g = LOOPED + k - LOGW - 1
                if g < GROUPS:
                    h_products(pe, g, g % 2)

            pe.wait_ge(s_dec, DECODED)
            pe.matmul(cnt_ps, zeros_p, zeros_i, start=True, stop=False, skip_group_check=True).then_inc(s_hot_free, 2)
            with pe.Fori(0, BODIES) as i:
                for h in range(2):
                    pe.wait_ge(s_hot, 2 * i + h + 1)
                    for r in range(HR):
                        ins = pe.matmul(cnt_ps, hot_p[:, h, r, :], hot_i[:, h, r, :], start=False, stop=False,
                                        skip_group_check=True)
                    ins.then_inc(s_hot_free, 1)

            pe.wait_ge(s_fix, 1)
            pe.matmul(wrow_ps, ones, w_diag, start=True, stop=True).then_inc(s_zt, 1)
            pe.wait_ge(s_acc, 1 + ROUNDS)
            for c in range(DC):
                ins = pe.transpose(z_ps[:, c * P:(c + 1) * P], state[:, c * P:(c + 1) * P], ident)
            ins.then_inc(s_zt, 1)
            pe.wait_ge(s_fix, 5)
            for c in range(DC):
                ins = pe.transpose(carry_ps[:, c * P:(c + 1) * P], carry_t[:, c, 0:P], ident)
            ins.then_inc(s_zt, 1)
            pe.wait_ge(s_cnt, 2)
            pe.matmul(off_ps, tri, incl[:, NT - 1:NT], start=True, stop=True).then_inc(s_off, 1)

            def turn(g, s, j):
                slot = (s * HG + j) % 2
                pe.wait_ge(s_agg[s * HG + j], 8 * (g - s) + 16)
                pe.wait_ge(s_at_c, g * HG + j + 1)
                for c in range(DC):
                    ins = pe.transpose(xt_ps[:, slot, c * P:(c + 1) * P], agg[s][:, j, c * P:(c + 1) * P], ident)
                ins.then_inc(s_at, 1)

            def product(g, s, j):
                slot = (s * HG + j) % 2
                pe.wait_ge(s_at_c, g * HG + j + 3)
                pe.wait_ge(s_sum, g * HG + j + 1)
                for c in range(DC):
                    ins = pe.matmul(mm_ps[0:NP, slot, 0:D], xt[:, slot, c, 0:NP], w2[:, c, :],
                                    start=(c == 0), stop=(c == DC - 1))
                ins.then_inc(s_y, 1)

            pe.wait_ge(s_fix, FIX_DONE)
            with pe.Fori(0, GROUPS // 2) as b:
                for s in range(2):
                    g = 2 * b + s
                    turn(g, s, 0)
                    for j in range(HG):
                        if j + 1 < HG:
                            turn(g, s, j + 1)
                        product(g, s, j)

        @block.scalar
        def _(act):
            act.sem_inc(s_xt_c, 2)
            act.sem_inc(s_h, 2)
            act.sem_inc(s_at_c, 2)
            for s in range(2):
                h_evacuate(act, s, s)
            with act.Fori(1, LOOPED // 2) as b:
                for s in range(2):
                    h_evacuate(act, 2 * b + s, s)
            for k in range(LOGW + 1, LOGN + 1):
                act.wait_ge(s_sort, level_end[k - 1])
                for q in range(4):
                    cols = slice(q * W // 4, (q + 1) * W // 4)
                    act.mul(signed[:, cols], keys[held[k - 1]][:, cols],
                            cst[:, C_SIGN + k - LOGW:C_SIGN + k - LOGW + 1]).then_inc(s_signed, 1)
                for h in range(2):
                    act.wait_ge(s_tr, level_base(k, 4) + h + 1)
                    act.copy(upper[:, h * HALF // 2:(h + 1) * HALF // 2].rearrange("p (a d) -> p a d", d=1 << (k - LOGW - 1)),
                             pairs(tp[:, h * HALF:(h + 1) * HALF], 1 << (k - LOGW - 1))[1]).then_inc(s_up, 1)
                act.wait_ge(s_tr, level_base(k, 4) + 3)
                act.copy(upper, bp[:, HALF:W]).then_inc(s_up, 1)
                g = LOOPED + k - LOGW - 1
                if g < GROUPS:
                    h_evacuate(act, g, g % 2)

            def stage(h, t):
                act.copy(nbr_now[:, h, :], nbr[:, bass.ds(t, HR)])
                act.copy(same_now[:, h, :], same[:, bass.ds(t, HR)]).then_inc(s_staged, 1)

            act.wait_ge(s_dec, 5)
            for h in range(2):
                stage(h, h * HR)
            with act.Fori(0, BODIES - 1) as i:
                for h in range(2):
                    act.wait_ge(s_acc, 1 + 2 * HR * i + (h + 1) * HR)
                    stage(h, 2 * HR * (i + 1) + h * HR)

            def deviation(g, s):
                act.wait_ge(s_var, g + 1)
                act.activation(std[0:NP, s, :], mv[0:NP, s, :, 1], ACT.Sqrt, bias=eps[0:NP, :]).then_inc(s_std, 1)

            def normalise(g, s, tiles):
                if tiles[0] == 0:
                    act.wait_ge(s_scale, g + 1)
                    if not (isinstance(g, int) and g < 2):
                        act.wait_ge(s_out[s], 16 * (g - s))
                for j in tiles:
                    ins = act.activation(o_buf[s][0:NP, j, :], y_buf[s][0:NP, j, :], ACT.Identity,
                                         bias=shift[0:NP, s, j:j + 1], scale=rstd[0:NP, s, j:j + 1])
                if tiles[-1] == HG - 1:
                    ins.then_inc(s_norm, 1)

            def tail_group(g, s, with_last):
                if with_last:
                    deviation(g - 1, 1 - s)
                for j in range(HG):
                    copy_turned(act, s_at, s_at_c, g * HG + j, (s * HG + j) % 2)
                    if with_last and j >= 2:
                        normalise(g - 1, 1 - s, [[0, 1], [2, 3], [4]][j - 2])

            for g in range(3):
                tail_group(g, g % 2, g > 0)
            with act.Fori(1, GROUPS // 2 - 1) as b:
                tail_group(2 * b + 1, 1, True)
                tail_group(2 * b + 2, 0, True)
            tail_group(GROUPS - 1, 1, True)
            deviation(GROUPS - 1, 1)
            normalise(GROUPS - 1, 1, list(range(HG)))

        @block.vector
        def _(dve):
            dve.sem_inc(s_sum, 2)
            dve.memset(state, 0.0).then_inc(s_acc, 1)

            dve.memset(keys[1], PAD_KEY).then_inc(s_sort, 1)
            dve.wait_ge(s_sort, 1)
            dve.wait_ge(s_edges, 32)
            dve.tensor_scalar(key_bits[0:NP, 0:EC], src_in[0:NP, :], DST_BITS, MARK, ALU.logical_shift_left,
                              ALU.bitwise_or).then_inc(s_sort, 1)
            dve.wait_ge(s_sort, 2)
            dve.tensor_tensor(key_bits[0:NP, 0:EC], key_bits[0:NP, 0:EC], dst_in[0:NP, :], ALU.bitwise_or).then_inc(s_sort, 1)
            dve.wait_ge(s_sort, 3)
            dve.wait_ge(s_consts, 16)
            dve.tensor_scalar(keys[0], keys[1], cst[:, C_SIGN:C_SIGN + 1], None, ALU.mult).then_inc(s_sort, 1)

            steps = SETUP
            cur = 0

            def exchange(low, high, out_low, out_high):
                nonlocal steps
                dve.wait_ge(s_sort, steps)
                dve.tensor_tensor(out_low, low, high, ALU.min)
                dve.tensor_tensor(out_high, low, high, ALU.max).then_inc(s_sort, 1)
                steps += 1

            def columns_apart(d):
                nonlocal cur
                exchange(*pairs(keys[cur], d), *pairs(keys[1 - cur], d))
                cur = 1 - cur

            for k in range(1, LOGW + 1):
                d = 1 << (k - 1)
                low, high = pairs(keys[cur], d)
                out_low, out_high = pairs(keys[1 - cur], d)
                exchange(low, high[:, :, ::-1], out_low, out_high[:, :, ::-1])
                cur = 1 - cur
                for e in range(k - 2, -1, -1):
                    columns_apart(1 << e)
            for k in range(LOGW + 1, LOGN + 1):
                d = 1 << (k - LOGW - 1)
                for h in range(2):
                    dve.wait_ge(s_up, level_base(k, 3) + h + 1)
                    half = slice(h * HALF, (h + 1) * HALF)
                    exchange(pairs(tp[:, half], d)[0],
                             upper[:, h * HALF // 2:(h + 1) * HALF // 2].rearrange("p (a d) -> p a d", d=d),
                             *pairs(keys[1 - cur][:, half], d))
                cur = 1 - cur
                for e in range(k - LOGW - 2, -1, -1):
                    columns_apart(1 << e)
                dve.wait_ge(s_tr, level_base(k, 4) + 4)
                dve.wait_ge(s_up, level_base(k, 3) + 3)
                exchange(bp[:, 0:HALF], upper, keys[1 - cur][:, 0:HALF], keys[1 - cur][:, HALF:W])
                cur = 1 - cur
                for e in range(LOGW - 2, -1, -1):
                    columns_apart(1 << e)
            assert steps == SORTED and cur == held[LOGN]

            def linked(semaphore, start=0):
                count = start

                def link(ins):
                    nonlocal count
                    count += 1
                    ins.then_inc(semaphore, 1)
                    dve.wait_ge(semaphore, count)
                return link

            link = linked(s_dec)
            dve.wait_ge(s_srt, 32)
            bits = srt[:, :].bitcast(I32)
            link(dve.tensor_scalar(seg[:, :], bits, DST_BITS, None, ALU.logical_shift_right))
            link(dve.tensor_scalar(nbr[:, :], bits[:, 1:], (1 << DST_BITS) - 1, None, ALU.bitwise_and))
            link(dve.tensor_tensor(same[:, :], seg[:, 1:], seg[:, 0:ROUNDS], ALU.is_equal))
            link(dve.tensor_copy(col[:, CONT:CONT + 1], same[:, 0:1]))
            link(dve.memset(same[:, 0:1], 0.0))
            link(dve.tensor_scalar(node_f, seg[:, 1:], float(-SEG0), None, ALU.add))
            link(dve.tensor_scalar(node_t, node_f, 1.0 / NT, -(NT - 1) / (2.0 * NT), ALU.mult, ALU.add))
            link(dve.tensor_scalar(node_t, node_t, ROUNDER, None, ALU.add))
            link(dve.tensor_scalar(node_t, node_t, -ROUNDER, None, ALU.add))
            link(dve.tensor_copy(node_p[:, :], node_t))
            link(dve.scalar_tensor_tensor(out=node_i[:, :], in0=node_t, scalar=float(-NT), in1=node_f,
                                          op0=ALU.mult, op1=ALU.add))
            link(dve.tensor_scalar(node_t, node_f, node_f[:, 0:1], 0.0, ALU.is_equal, ALU.add,
                                   accum_out=col[:, L_FIRST:L_FIRST + 1]))
            link(dve.tensor_scalar(col[:, WHOLE:WHOLE + 1], col[:, L_FIRST:L_FIRST + 1], float(ROUNDS), None, ALU.is_equal))
            link(dve.tensor_tensor(col[:, CARRY_ON:CARRY_ON + 1], col[:, WHOLE:WHOLE + 1], col[:, CONT:CONT + 1], ALU.mult))
            link(dve.tensor_tensor(first_at[:, :], col[:, L_FIRST:L_FIRST + 1], cst[:, C_ROW:C_ROW + 1], ALU.add))
            link(dve.memset(hot_p[:, 0, 0, :], 0.0))
            link(dve.memset(hot_i[:, 0, 0, :], 0.0))

            dve.wait_ge(s_wcat, 1)
            with dve.Fori(0, BODIES) as i:
                for h in range(2):
                    t0 = 2 * HR * i + HR * h
                    dve.wait_ge(s_hot_free, 2 * i + h + 1)
                    dve.tensor_tensor(hot_p[:, h, :, :], iota[:, :].unsqueeze(1).to_broadcast([P, HR, P]),
                                      node_p[:, bass.ds(t0, HR)].unsqueeze(2).to_broadcast([P, HR, P]), ALU.is_equal)
                    dve.tensor_tensor(hot_i[:, h, :, :], iota[:, 0:NT].unsqueeze(1).to_broadcast([P, HR, NT]),
                                      node_i[:, bass.ds(t0, HR)].unsqueeze(2).to_broadcast([P, HR, NT]),
                                      ALU.is_equal).then_inc(s_hot, 1)
                    dve.wait_ge(s_tab[h], 16 * i + 16)
                    for g, rounds in enumerate(GATHER_GROUPS):
                        dve.wait_ge(s_rows[h][g], 16 * len(rounds) * i + 16 * len(rounds))
                        for r in rounds:
                            dve.wait_ge(s_acc, t0 + r + 1)
                            slot = h * HR + r
                            dve.scalar_tensor_tensor(out=runmax[:, slot, :], in0=runmax[:, slot - 1 if slot else 2 * HR - 1, :],
                                                     scalar=same_now[:, h, r:r + 1], in1=ring[:, slot, :],
                                                     op0=ALU.mult, op1=ALU.max).then_inc(s_acc, 1)
            dve.wait_ge(s_acc, 1 + ROUNDS)

            fix = linked(s_fix)
            fix(dve.tensor_scalar(w_diag, ident, col[:, CARRY_ON:CARRY_ON + 1], None, ALU.mult))
            dve.wait_ge(s_zt, 1)
            fix(dve.tensor_copy(w_row, wrow_ps))
            fix(dve.memset(carry_t[:, :, 0:1], 0.0))
            dve.wait_ge(s_zt, 2)
            for c in range(DC):
                fix(dve.tensor_tensor_scan(carry_t[:, c, 1:P + 1], w_row, z_ps[:, c * P:(c + 1) * P], 0.0, ALU.mult, ALU.max))

            link = linked(s_cnt)
            dve.wait_ge(s_hot_free, 2 + 2 * BODIES)
            link(dve.tensor_copy(cnt, cnt_ps))
            link(dve.tensor_tensor_scan(incl, ones[:, 0:NT], cnt, 0.0, ALU.mult, ALU.add))
            dve.wait_ge(s_off, 1)
            link(dve.tensor_copy(col[:, OFF:OFF + 1], off_ps))
            link(dve.tensor_scalar(last, incl, col[:, OFF:OFF + 1], -1.0, ALU.add, ALU.add))
            link(dve.tensor_tensor(first, last, cnt, ALU.subtract))
            middle = (ROUNDS - 1) / 2.0
            link(dve.tensor_scalar(e_p, last, 1.0 / ROUNDS, -middle / ROUNDS, ALU.mult, ALU.add))
            link(dve.tensor_scalar(e_p, e_p, ROUNDER, None, ALU.add))
            link(dve.tensor_scalar(e_p, e_p, -ROUNDER, None, ALU.add))
            link(dve.tensor_scalar(s_p, first, 1.0 / ROUNDS, (1 - middle) / ROUNDS, ALU.mult, ALU.add))
            link(dve.tensor_scalar(s_p, s_p, ROUNDER, None, ALU.add))
            link(dve.tensor_scalar(s_p, s_p, -ROUNDER, None, ALU.add))
            link(dve.tensor_tensor(t_a, e_p, s_p, ALU.not_equal))
            link(dve.tensor_tensor(t_b, e_p, last, ALU.subtract))
            link(dve.scalar_tensor_tensor(out=t_b, in0=t_b, scalar=float(FIX0), in1=t_a, op0=ALU.add, op1=ALU.mult))
            link(dve.tensor_tensor(last, last, t_b, ALU.add))
            link(dve.tensor_scalar(t_a, cnt, 0.0, None, ALU.is_equal))
            link(dve.tensor_scalar(t_b, last, -1.0, float(ZERO_ROW), ALU.mult, ALU.add))
            link(dve.tensor_tensor(t_b, t_b, t_a, ALU.mult))
            link(dve.tensor_tensor(node_at[:, :], last, t_b, ALU.add))

            dve.wait_ge(s_zt, 3)
            dve.wait_ge(s_first, 16)
            dve.scalar_tensor_tensor(out=fix_rows, in0=carry_ps, scalar=col[:, CONT:CONT + 1], in1=first_rows,
                                     op0=ALU.mult, op1=ALU.max).then_inc(s_fix, 1)

            def scales(g, s):
                dve.wait_ge(s_std, g + 1)
                dve.reciprocal(rstd[0:NP, s, :], std[0:NP, s, :]).then_inc(s_rstd, 1)
                dve.wait_ge(s_rstd, g + 1)
                dve.scalar_tensor_tensor(out=shift[0:NP, s, :], in0=mv[0:NP, s, :, 0], scalar=-1.0, in1=rstd[0:NP, s, :],
                                         op0=ALU.mult, op1=ALU.mult).then_inc(s_scale, 1)

            def tail_group(g, s, with_last):
                def add(j):
                    n = g * HG + j
                    dve.wait_ge(s_y, n + 1)
                    dve.tensor_tensor(y_buf[s][0:NP, j, :], mm_ps[0:NP, (s * HG + j) % 2, 0:D],
                                      base_flat[0:NP, bass.ds(n * D, D)], ALU.add).then_inc(s_sum, 1)

                def statistics(j):
                    dve.wait_ge(s_sum, g * HG + j + 3)
                    dve.bn_stats(stats[0:NP, s, j, :], y_buf[s][0:NP, j, :]).then_inc(s_stat, 1)

                if not (isinstance(g, int) and g < 2):
                    dve.wait_ge(s_norm, g - 1)
                add(0)
                for j in range(HG):
                    if j + 1 < HG:
                        add(j + 1)
                    statistics(j)
                    if with_last and j == 1:
                        scales(g - 1, 1 - s)
                dve.wait_ge(s_stat, g * HG + HG)
                dve.sem_inc(s_seen, 1)
                for j in range(HG):
                    ins = dve.bn_aggr(mv[0:NP, s, j, :], stats[0:NP, s, j, :])
                ins.then_inc(s_var, 1)

            for h in range(2):
                dve.wait_ge(s_tab[h], 16 + 16 * BODIES)
            for g in range(3):
                tail_group(g, g % 2, g > 0)
            with dve.Fori(1, GROUPS // 2 - 1) as b:
                tail_group(2 * b + 1, 1, True)
                tail_group(2 * b + 2, 0, True)
            tail_group(GROUPS - 1, 1, True)
            scales(GROUPS - 1, 1)


def kernel(x, src, dst, L0_gnn_fc_w, L0_gnn_fc_b, L0_gnn_weights_matrix):
    import numpy as np
    import concourse.bacc as bacc
    from concourse.bass_utils import run_bass_kernel_spmd

    p = np.arange(P)
    consts = np.zeros((P, C_ALL), np.float32)
    consts[:, C_ID:C_ID + P] = np.eye(P)
    consts[:, C_TRI:C_TRI + P] = p[:, None] < p[None, :]
    consts[:, C_IOTA:C_IOTA + P] = p[None, :]
    down = [(p >> n) & 1 for n in range(8)]
    for n in range(8):
        consts[:, C_SIGN + n] = 1 - 2 * (down[n] if n == 0 else down[n] ^ down[n - 1])
    consts[:, C_ROW] = p * ROUNDS - 1
    consts[:, C_ONE:C_ONE + P] = 1

    given = {"x": x, "src": src, "dst": dst, "fc_w": L0_gnn_fc_w, "fc_b": L0_gnn_fc_b,
             "wm": L0_gnn_weights_matrix, "consts": consts}
    nc = bacc.Bacc("TRN2", target_bir_lowering=False, num_devices=1)
    arrays, args = {}, []
    for name, a in given.items():
        a = np.ascontiguousarray(a)
        arrays[f"in_{name}"] = a
        args.append(nc.dram_tensor(f"in_{name}", a.shape, mybir.dt.from_np(a.dtype), kind="ExternalInput").ap())
    out = nc.dram_tensor("out_y", (NODES, D), F32, kind="ExternalOutput").ap()
    build(nc, *args, out)
    return run_bass_kernel_spmd(nc, [arrays], core_ids=[0]).results[0]["out_y"]
```

```python
from contextlib import ExitStack

import concourse.bass as bass
from concourse import mybir

ALU = mybir.AluOpType
ACT = mybir.ActivationFunctionType
F32 = mybir.dt.float32
BF16 = mybir.dt.bfloat16
I32 = mybir.dt.int32

P = 128
D = 256
DC = D // P
NODES = 6250
NP = 125
NT = NODES // NP
SPREAD = 112
EDGES = 100000
EC = EDGES // NP

LOGW = 10
W = 1 << LOGW
LOGN = LOGW + 7
HALF = W // 2
DST_BITS = 13
MARK = 0x20000000
PAD_KEY = float(2.0 ** 127)
SEG0 = MARK >> DST_BITS
LEAD = 64

ROUNDS = -(-EDGES // P)
HR = 17
BODIES = ROUNDS // (2 * HR)
GATHER_GROUPS = [range(0, 4), range(4, 8), range(8, 12), range(12, 15), range(15, HR)]
STORE_PARTS = [(0, 8), (8, 14), (14, HR)]
FIX0 = P * ROUNDS
ZERO_ROW = FIX0 + P
TABLE = ZERO_ROW + 1
ROUNDER = float(3 << 22)

HG = 5
GROUPS = NT // HG
LOOPED = 4
NORM_LAG = 2 * HG
EPS = 1e-5

C_ID, C_TRI, C_IOTA, C_SIGN, C_ROW, C_ONE = 0, P, 2 * P, 3 * P, 3 * P + 8, 4 * P
C_ALL = 5 * P


def build(nc, x, src, dst, fc_w, fc_b, wm, consts, out):
    assert NP * NT == NODES and NP * EC == EDGES and 2 * HR * BODIES == ROUNDS and EC <= W
    ctx = ExitStack()
    with ctx:
        def sb(name, shape, dt):
            return ctx.enter_context(nc.sbuf_tensor(name, shape, dt))

        def ps(name, shape):
            return ctx.enter_context(nc.psum_tensor(name, shape, F32))

        def sem(name):
            return ctx.enter_context(nc.semaphore(name))

        keys_dram = nc.dram_tensor("sorted_keys", [LEAD + P * W], F32).ap()
        h_dram = nc.dram_tensor("h_rows", [NODES, D], F32).ap()
        table = nc.dram_tensor("running_max", [TABLE, D], F32).ap()
        table_rounds = table[0:FIX0, :].rearrange("(p c) f -> p c f", c=ROUNDS)

        base = sb("base", [P, NT * D], F32)
        cst = sb("cst", [P, C_ALL], F32)
        w_cat = sb("w_cat", [P, DC, 2 * D], F32)
        w2 = sb("w2", [P, DC, D], F32)
        bias = sb("bias", [1, D], F32)
        xt = sb("xt", [P, 2, DC, P], F32)
        ring = sb("ring", [P, 2 * HR, D], F32)
        runmax = sb("runmax", [P, 2 * HR, D], F32)
        srt = sb("srt", [P, ROUNDS + 1], F32)
        seg = sb("seg", [P, ROUNDS + 1], I32)
        nbr = sb("nbr", [P, ROUNDS], I32)
        same = sb("same", [P, ROUNDS], F32)
        node_p = sb("node_p", [P, ROUNDS], BF16)
        node_i = sb("node_i", [P, ROUNDS], BF16)
        nbr_now = sb("nbr_now", [P, 2, HR], I32)
        same_now = sb("same_now", [P, 2, HR], F32)
        iota = sb("iota", [P, P], BF16)
        hot_p = sb("hot_p", [P, 2, HR, P], BF16)
        hot_i = sb("hot_i", [P, 2, HR, NT], BF16)
        col = sb("col", [P, 16], F32)
        first_at = sb("first_at", [P, 1], I32)
        node_at = sb("node_at", [P, NT], I32)
        stats = sb("stats", [P, 2, HG, 6], F32)
        mv = sb("mv", [P, 2, HG, 2], F32)
        std = sb("std", [P, NT], F32)
        rstd = sb("rstd", [P, NT], F32)
        shift = sb("shift", [P, NT], F32)
        eps = sb("eps", [P, 1], F32)
        w_diag = sb("w_diag", [P, P], F32)
        w_row = sb("w_row", [P, P], F32)
        carry_t = sb("carry_t", [P, DC, P + 1], F32)

        flat = ring[:, :, :].rearrange("p a b -> p (a b)")
        keys = [flat[:, 0:W], flat[:, W:2 * W]]
        signed = flat[:, 2 * W:3 * W]
        upper = flat[:, 3 * W:3 * W + HALF]
        src_in = flat[:, 4 * W:4 * W + EC].bitcast(I32)
        dst_in = flat[:, 5 * W:5 * W + EC].bitcast(I32)
        key_bits = keys[1].bitcast(I32)
        flat_max = runmax[:, :, :].rearrange("p a b -> p (a b)")
        node_f = flat_max[:, 20 * D:20 * D + ROUNDS]
        node_t = flat_max[:, 24 * D:24 * D + ROUNDS]
        xg = [runmax[:, s * HG:(s + 1) * HG, :] for s in range(2)]
        hg = [runmax[:, (2 + s) * HG:(3 + s) * HG, :] for s in range(2)]
        first_rows = ring[:, 20, :]
        fix_rows = ring[:, 21, :]
        cnt, incl, last, first, e_p, s_p, t_a, t_b = (
            flat[:, 27 * D + n * 64:27 * D + n * 64 + NT] for n in range(8))
        agg = [ring[:, s * HG:(s + 1) * HG, :] for s in range(2)]

        tp = ps("tp", [P, W])
        bp = ps("bp", [P, W])
        xt_ps = ps("xt_ps", [P, 2, 512])
        mm_ps = ps("mm_ps", [P, 2, 512])
        cnt_ps = tp[:, 0:NT]
        off_ps = tp[:, HALF:HALF + 1]
        z_ps = bp[:, 0:D]
        wrow_ps = bp[:, HALF:HALF + P]
        carry_ps = xt_ps[:, 0, 0:D]

        ident = cst[:, C_ID:C_ID + P]
        tri = cst[:, C_TRI:C_TRI + P]
        ones = cst[:, C_ONE:C_ONE + P]
        L_FIRST, CONT, WHOLE, CARRY_ON, OFF = range(5)

        s_edges = sem("edges_loaded")
        s_consts = sem("consts_loaded")
        s_weights = sem("weights_loaded")
        s_x = [sem(f"x_loaded_{s}") for s in range(2)]
        s_wcat = sem("w_cat_ready")
        s_xt_t = sem("x_transposed")
        s_xt_c = sem("xt_copied")
        s_mm = sem("h_product_done")
        s_h = sem("h_evacuated")
        s_h_st = [sem(f"h_stored_{s}") for s in range(2)]
        s_sort = sem("sort_steps")
        s_signed = sem("signed_pieces")
        s_tr = sem("sort_transposes")
        s_up = sem("upper_copied")
        s_keys_st = sem("keys_stored")
        s_lead = sem("lead_stored")
        s_srt = sem("sorted_loaded")
        s_dec = sem("decoded")
        s_pre = sem("vector_setup")
        s_staged = sem("halves_staged")
        s_pool = sem("pool_halves")
        s_rows = [[sem(f"rows_{h}_{g}") for g in range(len(GATHER_GROUPS))] for h in range(2)]
        s_acc = sem("rounds_done")
        s_tab = [sem(f"table_stored_{h}") for h in range(2)]
        s_hot = sem("onehots_ready")
        s_hot_free = sem("onehots_free")
        s_cnt = sem("count_steps")
        s_off = sem("offsets_ready")
        s_first = sem("first_rows_loaded")
        s_zt = sem("carry_transposes")
        s_fix = sem("fix_steps")
        s_fix_st = sem("fix_rows_stored")
        s_agg = [sem(f"agg_loaded_{j}") for j in range(2 * HG)]
        s_at = sem("agg_transposed")
        s_at_c = sem("agg_copied")
        s_y = sem("agg_product_done")
        s_sum = sem("y_summed")
        s_stat = sem("statistics_ready")
        s_seen = sem("statistics_seen")
        s_var = sem("variance_ready")
        s_std = sem("deviation_ready")
        s_rstd = sem("rstd_ready")
        s_scale = sem("scales_ready")
        s_norm = sem("tiles_normed")
        s_last = sem("last_group_normed")
        s_out = sem("out_stored")

        PARTS = (slice(0, SPREAD), slice(SPREAD, NP))
        x_tiles = x.rearrange("(p i) f -> p i f", i=NT)
        h_tiles = h_dram.rearrange("(p i) f -> p i f", i=NT)
        out_rows = out.rearrange("(p i) f -> p (i f)", i=NT)

        SETUP = 4
        IN_PART = LOGW * (LOGW + 1) // 2
        level_end = {LOGW: SETUP + IN_PART}
        for k in range(LOGW + 1, LOGN + 1):
            level_end[k] = level_end[k - 1] + k + 1
        SORTED = level_end[LOGN]
        held = {LOGW: IN_PART % 2}
        for k in range(LOGW + 1, LOGN + 1):
            held[k] = (held[k - 1] + k) % 2

        def turned_end(k):
            return level_end[k - 1] + (k - LOGW) + 1

        def turned_held(k):
            return (held[k - 1] + k - LOGW) % 2

        state = runmax[:, 2 * HR - 1, :]
        zeros_p, zeros_i = hot_p[:, 0, 0, :], hot_i[:, 0, 0, :]
        FIX_DONE = 6
        CNT_DONE = 19
        DECODED = 17

        block = ctx.enter_context(nc.Block())

        @block.sync
        def _(sp):
            sp.dma_start(src_in[0:NP, :], src.rearrange("(p c) -> p c", c=EC)).then_inc(s_edges, 16)
            sp.dma_start(dst_in[0:NP, :], dst.rearrange("(p c) -> p c", c=EC)).then_inc(s_edges, 16)
            sp.dma_start(cst[:, :], consts).then_inc(s_consts, 16)

            def load_x(g):
                for part in PARTS:
                    sp.dma_start(xg[g % 2][part, :, :], x_tiles[part, g * HG:(g + 1) * HG, :]).then_inc(s_x[g % 2], 16)

            load_x(0)
            sp.dma_start(w_cat[:, :, 0:D], fc_w.rearrange("(c p) n -> p c n", c=DC)).then_inc(s_weights, 16)
            sp.dma_start(w_cat[:, :, D:2 * D], wm[0:D, :].rearrange("(c p) n -> p c n", c=DC)).then_inc(s_weights, 16)
            sp.dma_start(w2[:, :, :], wm[D:2 * D, :].rearrange("(c p) n -> p c n", c=DC)).then_inc(s_weights, 16)
            sp.dma_start(bias[:, :], fc_b.rearrange("(a n) -> a n", a=1)).then_inc(s_weights, 16)
            load_x(1)
            sp.wait_ge(s_consts, 16)
            sp.dma_start(keys_dram[LEAD - 1:LEAD].rearrange("(a n) -> a n", a=1),
                         cst[0:1, C_IOTA:C_IOTA + 1]).then_inc(s_lead, 16)
            sp.wait_ge(s_acc, 1)
            for h in range(2):
                sp.dma_start(table[ZERO_ROW:ZERO_ROW + 1, h * P:(h + 1) * P], state[0:1, h * P:(h + 1) * P]).then_inc(s_tab[h], 16)
            for g in range(GROUPS):
                sp.wait_ge(s_h, 2 + HG * (g + 1))
                for part in PARTS:
                    sp.dma_start(h_tiles[part, g * HG:(g + 1) * HG, :], hg[g % 2][part, :, :]).then_inc(s_h_st[g % 2], 16)
                if g + 2 < GROUPS:
                    sp.wait_ge(s_xt_t, HG * (g + 1))
                    load_x(g + 2)
            sp.wait_ge(s_sort, SORTED)
            sp.dma_start(keys_dram[LEAD:LEAD + P * W].rearrange("(p c) -> p c", c=W), keys[held[LOGN]]).then_inc(s_keys_st, 16)
            sp.wait_ge(s_keys_st, 16)
            sp.wait_ge(s_lead, 16)
            chunks = keys_dram[LEAD - 1:LEAD - 1 + P * ROUNDS].rearrange("(p c) -> p c", c=ROUNDS)
            sp.dma_start(srt[:, 0:ROUNDS], chunks).then_inc(s_srt, 16)
            ends = keys_dram[LEAD - 1 + ROUNDS:LEAD - 1 + ROUNDS + P * ROUNDS].rearrange("(p c) -> p c", c=ROUNDS)
            sp.dma_start(srt[:, ROUNDS:ROUNDS + 1], ends[:, 0:1], allow_slow_non_contiguous=True).then_inc(s_srt, 16)
            with sp.Fori(0, BODIES) as i:
                for h in range(2):
                    for a, e in STORE_PARTS:
                        sp.wait_ge(s_acc, 1 + 2 * HR * i + HR * h + e)
                        sp.dma_start(table_rounds[:, bass.ds(2 * HR * i + HR * h + a, e - a), :],
                                     runmax[:, h * HR + a:h * HR + e, :]).then_inc(s_tab[h], 16)
            sp.wait_ge(s_fix, FIX_DONE)
            sp.dma_start(table[FIX0:FIX0 + P, :], fix_rows).then_inc(s_fix_st, 16)

            def store(g):
                for part in PARTS:
                    sp.dma_start(out_rows[part, bass.ds(g * HG * D, HG * D)],
                                 base[part, bass.ds(g * HG * D, HG * D)]).then_inc(s_out, 16)

            with sp.Fori(0, GROUPS - 1) as g:
                sp.wait_ge(s_norm, g * HG + HG)
                store(g)
            sp.wait_ge(s_last, HG)
            store(GROUPS - 1)
            sp.wait_ge(s_out, 32 * GROUPS)
            for s in range(2):
                sp.wait_ge(s_h_st[s], 32 * (GROUPS // 2))

        @block.gpsimd
        def _(pool):
            pool.wait_ge(s_consts, 16)
            pool.wait_ge(s_weights, 64)
            for c in range(DC):
                diag = w_cat[:, c, D + c * P:D + (c + 1) * P]
                pool.tensor_tensor(diag, diag, ident, ALU.add)
            pool.tensor_copy(iota[:, :], cst[:, C_IOTA:C_IOTA + P])
            pool.memset(eps[:, :], EPS).then_inc(s_wcat, 1)
            for s in range(2):
                pool.wait_ge(s_h_st[s], 32 * (GROUPS // 2))
            with pool.Fori(0, BODIES) as i:
                for h in range(2):
                    pool.wait_ge(s_staged, 2 * i + h + 1)
                    pool.sem_inc(s_pool, 1)
                    for g, rounds in enumerate(GATHER_GROUPS):
                        for r in rounds:
                            pool.indirect_dma_start(
                                ring[:, h * HR + r, :], None, h_dram,
                                bass.IndirectOffsetOnAxis(ap=nbr_now[:, h, r:r + 1], axis=0)).then_inc(s_rows[h][g], 16)
            for h in range(2):
                pool.wait_ge(s_tab[h], 16 + 16 * len(STORE_PARTS) * BODIES)
            pool.indirect_dma_start(first_rows, None, table[0:FIX0, :],
                                    bass.IndirectOffsetOnAxis(ap=first_at[:, :], axis=0)).then_inc(s_first, 16)
            pool.wait_ge(s_cnt, CNT_DONE)
            pool.wait_ge(s_fix_st, 16)
            for t in range(NT):
                if t >= 2 * HG:
                    pool.wait_ge(s_at, t - 2 * HG + 1)
                pool.indirect_dma_start(agg[t // HG % 2][:, t % HG, :], None, table,
                                        bass.IndirectOffsetOnAxis(ap=node_at[:, t:t + 1], axis=0)).then_inc(s_agg[t % (2 * HG)], 16)

        def h_products(pe, g, s):
            def turn(j):
                slot = (s * HG + j) % 2
                if j == 0:
                    pe.wait_ge(s_x[s], 16 * (g - s) + 32)
                pe.wait_ge(s_xt_c, g * HG + j + 1)
                for c in range(DC):
                    ins = pe.transpose(xt_ps[:, slot, c * P:c * P + NP], xg[s][0:NP, j, c * P:(c + 1) * P],
                                       ident[0:NP, 0:NP])
                ins.then_inc(s_xt_t, 1)

            def product(j):
                slot = (s * HG + j) % 2
                pe.wait_ge(s_xt_c, g * HG + j + 3)
                pe.wait_ge(s_h, g * HG + j + 1)
                for c in range(DC):
                    pe.matmul(mm_ps[0:NP, slot, :], xt[:, slot, c, 0:NP], w_cat[:, c, :], start=(c == 0), stop=False,
                              skip_group_check=True)
                pe.matmul(mm_ps[0:NP, slot, 0:D], ones[0:1, 0:NP], bias[0:1, :], start=False, stop=True,
                          skip_group_check=True).then_inc(s_mm, 1)

            turn(0)
            for j in range(HG):
                if j + 1 < HG:
                    turn(j + 1)
                product(j)

        def copy_turned(act, turned, copied, n, slot):
            act.wait_ge(turned, n + 1)
            act.copy(xt[:, slot, :, 0:NP],
                     xt_ps[:, slot, 0:D].rearrange("p (c n) -> p c n", c=DC)[:, :, 0:NP]).then_inc(copied, 1)

        def h_evacuate(act, g, s):
            copy_turned(act, s_xt_t, s_xt_c, g * HG, s * HG % 2)
            for j in range(HG):
                slot = (s * HG + j) % 2
                if j + 1 < HG:
                    copy_turned(act, s_xt_t, s_xt_c, g * HG + j + 1, 1 - slot)
                act.wait_ge(s_mm, g * HG + j + 1)
                if j == 0 and not (isinstance(g, int) and g < 2):
                    act.wait_ge(s_h_st[s], 16 * (g - s))
                act.activation(hg[s][0:NP, j, :], mm_ps[0:NP, slot, 0:D], ACT.Relu)
                act.copy(base[0:NP, bass.ds((g * HG + j) * D, D)], mm_ps[0:NP, slot, D:2 * D]).then_inc(s_h, 1)

        def level_base(k, per_level):
            return per_level * (k - LOGW - 1)

        def pairs(buf, d):
            v = buf.rearrange("p (a two d) -> p a two d", two=2, d=d)
            return v[:, :, 0, :], v[:, :, 1, :]

        @block.tensor
        def _(pe):
            pe.wait_ge(s_wcat, 1)
            for s in range(2):
                h_products(pe, s, s)
            with pe.Fori(1, LOOPED // 2) as b:
                for s in range(2):
                    h_products(pe, 2 * b + s, s)
            for k in range(LOGW + 1, LOGN + 1):
                for b in range(W // P):
                    if b % 2 == 0:
                        pe.wait_ge(s_signed, level_base(k, 4) + b // 2 + 1)
                    ins = pe.transpose(tp[:, b * P:(b + 1) * P], signed[:, b * P:(b + 1) * P], ident)
                    if b % 4 == 3:
                        ins.then_inc(s_tr, 1)
                pe.wait_ge(s_sort, turned_end(k))
                for b in (4, 5, 6, 7, 0, 1, 2, 3):
                    ins = pe.transpose(bp[:, b * P:(b + 1) * P], keys[turned_held(k)][:, b * P:(b + 1) * P], ident)
                    if b % 4 == 3:
                        ins.then_inc(s_tr, 1)
                g = LOOPED + k - LOGW - 1
                if g < GROUPS:
                    h_products(pe, g, g % 2)

            pe.wait_ge(s_fix, 1)
            pe.matmul(wrow_ps, ones, w_diag[:, :], start=True, stop=True).then_inc(s_zt, 1)

            pe.wait_ge(s_dec, DECODED)
            pe.matmul(cnt_ps, zeros_p, zeros_i, start=True, stop=False, skip_group_check=True).then_inc(s_hot_free, 2)
            with pe.Fori(0, BODIES) as i:
                for h in range(2):
                    pe.wait_ge(s_hot, 2 * i + h + 1)
                    for r in range(HR):
                        ins = pe.matmul(cnt_ps, hot_p[:, h, r, :], hot_i[:, h, r, :], start=False, stop=False,
                                        skip_group_check=True)
                    ins.then_inc(s_hot_free, 1)

            pe.wait_ge(s_acc, 1 + ROUNDS)
            for c in range(DC):
                ins = pe.transpose(z_ps[:, c * P:(c + 1) * P], state[:, c * P:(c + 1) * P], ident)
            ins.then_inc(s_zt, 1)
            pe.wait_ge(s_fix, 5)
            for c in range(DC):
                ins = pe.transpose(carry_ps[:, c * P:(c + 1) * P], carry_t[:, c, 0:P], ident)
            ins.then_inc(s_zt, 1)
            pe.wait_ge(s_cnt, 2)
            pe.matmul(off_ps, tri, incl[:, NT - 1:NT], start=True, stop=True).then_inc(s_off, 1)

            def turn(g, s, j):
                slot = (s * HG + j) % 2
                pe.wait_ge(s_agg[s * HG + j], 8 * (g - s) + 16)
                pe.wait_ge(s_at_c, g * HG + j + 1)
                for c in range(DC):
                    ins = pe.transpose(xt_ps[:, slot, c * P:(c + 1) * P], agg[s][:, j, c * P:(c + 1) * P], ident)
                ins.then_inc(s_at, 1)

            def product(g, s, j):
                slot = (s * HG + j) % 2
                pe.wait_ge(s_at_c, g * HG + j + 3)
                pe.wait_ge(s_sum, g * HG + j + 1)
                for c in range(DC):
                    ins = pe.matmul(mm_ps[0:NP, slot, 0:D], xt[:, slot, c, 0:NP], w2[:, c, :],
                                    start=(c == 0), stop=(c == DC - 1))
                ins.then_inc(s_y, 1)

            pe.wait_ge(s_fix, FIX_DONE)
            with pe.Fori(0, GROUPS // 2) as b:
                for s in range(2):
                    g = 2 * b + s
                    turn(g, s, 0)
                    for j in range(HG):
                        if j + 1 < HG:
                            turn(g, s, j + 1)
                        product(g, s, j)

        @block.scalar
        def _(act):
            act.sem_inc(s_xt_c, 2)
            act.sem_inc(s_h, 2)
            act.sem_inc(s_at_c, 2)
            for s in range(2):
                h_evacuate(act, s, s)
            with act.Fori(1, LOOPED // 2) as b:
                for s in range(2):
                    h_evacuate(act, 2 * b + s, s)
            for k in range(LOGW + 1, LOGN + 1):
                act.wait_ge(s_sort, level_end[k - 1])
                for q in range(4):
                    cols = slice(q * W // 4, (q + 1) * W // 4)
                    act.mul(signed[:, cols], keys[held[k - 1]][:, cols],
                            cst[:, C_SIGN + k - LOGW:C_SIGN + k - LOGW + 1]).then_inc(s_signed, 1)
                for h in range(2):
                    act.wait_ge(s_tr, level_base(k, 4) + h + 1)
                    act.copy(upper[:, h * HALF // 2:(h + 1) * HALF // 2].rearrange("p (a d) -> p a d", d=1 << (k - LOGW - 1)),
                             pairs(tp[:, h * HALF:(h + 1) * HALF], 1 << (k - LOGW - 1))[1]).then_inc(s_up, 1)
                act.wait_ge(s_tr, level_base(k, 4) + 3)
                act.copy(upper, bp[:, HALF:W]).then_inc(s_up, 1)
                g = LOOPED + k - LOGW - 1
                if g < GROUPS:
                    h_evacuate(act, g, g % 2)

            def stage(h, t):
                act.copy(nbr_now[:, h, :], nbr[:, bass.ds(t, HR)])
                act.copy(same_now[:, h, :], same[:, bass.ds(t, HR)]).then_inc(s_staged, 1)

            act.wait_ge(s_dec, 5)
            for h in range(2):
                stage(h, h * HR)
            with act.Fori(0, BODIES - 1) as i:
                for h in range(2):
                    act.wait_ge(s_acc, 1 + 2 * HR * i + (h + 1) * HR)
                    stage(h, 2 * HR * (i + 1) + h * HR)

            def deviation(g, s):
                act.wait_ge(s_var, g + 1)
                act.activation(std[0:NP, bass.ds(g * HG, HG)], mv[0:NP, s, :, 1], ACT.Sqrt,
                               bias=eps[0:NP, :]).then_inc(s_std, 1)

            def normalise(n, scaled=None):
                if scaled is not None:
                    act.wait_ge(s_scale, scaled)
                y = base[0:NP, bass.ds(n * D, D)]
                act.activation(y, y, ACT.Identity, bias=shift[0:NP, bass.ds(n, 1)],
                               scale=rstd[0:NP, bass.ds(n, 1)]).then_inc(s_norm, 1)

            def tail_group(g, s, warm):
                for j in range(HG):
                    copy_turned(act, s_at, s_at_c, g * HG + j, (s * HG + j) % 2)
                    if j == 2 and warm > 0:
                        deviation(g - 1, 1 - s)
                    if warm > 1:
                        normalise(g * HG + j - NORM_LAG, g - 1 if j == 0 else None)

            tail_group(0, 0, 0)
            tail_group(1, 1, 1)
            with act.Fori(1, GROUPS // 2) as b:
                tail_group(2 * b, 0, 2)
                tail_group(2 * b + 1, 1, 2)
            for n in range(NT - NORM_LAG, NT - HG):
                if n == NT - HG - 2:
                    deviation(GROUPS - 1, 1)
                normalise(n, GROUPS - 1 if n == NT - NORM_LAG else None)

        @block.vector
        def _(dve):
            dve.sem_inc(s_sum, 2)
            dve.memset(state, 0.0).then_inc(s_acc, 1)

            dve.memset(keys[1], PAD_KEY).then_inc(s_sort, 1)
            dve.wait_ge(s_sort, 1)
            dve.wait_ge(s_edges, 32)
            dve.tensor_scalar(key_bits[0:NP, 0:EC], src_in[0:NP, :], DST_BITS, MARK, ALU.logical_shift_left,
                              ALU.bitwise_or).then_inc(s_sort, 1)
            dve.wait_ge(s_sort, 2)
            dve.tensor_tensor(key_bits[0:NP, 0:EC], key_bits[0:NP, 0:EC], dst_in[0:NP, :], ALU.bitwise_or).then_inc(s_sort, 1)
            dve.wait_ge(s_sort, 3)
            dve.wait_ge(s_consts, 16)
            dve.tensor_scalar(keys[0], keys[1], cst[:, C_SIGN:C_SIGN + 1], None, ALU.mult).then_inc(s_sort, 1)

            steps = SETUP
            cur = 0

            def exchange(low, high, out_low, out_high):
                nonlocal steps
                dve.wait_ge(s_sort, steps)
                dve.tensor_tensor(out_low, low, high, ALU.min)
                dve.tensor_tensor(out_high, low, high, ALU.max).then_inc(s_sort, 1)
                steps += 1

            def columns_apart(d):
                nonlocal cur
                exchange(*pairs(keys[cur], d), *pairs(keys[1 - cur], d))
                cur = 1 - cur

            for k in range(1, LOGW + 1):
                d = 1 << (k - 1)
                low, high = pairs(keys[cur], d)
                out_low, out_high = pairs(keys[1 - cur], d)
                exchange(low, high[:, :, ::-1], out_low, out_high[:, :, ::-1])
                cur = 1 - cur
                for e in range(k - 2, -1, -1):
                    columns_apart(1 << e)
            for k in range(LOGW + 1, LOGN + 1):
                d = 1 << (k - LOGW - 1)
                for h in range(2):
                    dve.wait_ge(s_up, level_base(k, 3) + h + 1)
                    half = slice(h * HALF, (h + 1) * HALF)
                    exchange(pairs(tp[:, half], d)[0],
                             upper[:, h * HALF // 2:(h + 1) * HALF // 2].rearrange("p (a d) -> p a d", d=d),
                             *pairs(keys[1 - cur][:, half], d))
                cur = 1 - cur
                for e in range(k - LOGW - 2, -1, -1):
                    columns_apart(1 << e)
                dve.wait_ge(s_tr, level_base(k, 4) + 4)
                dve.wait_ge(s_up, level_base(k, 3) + 3)
                exchange(bp[:, 0:HALF], upper, keys[1 - cur][:, 0:HALF], keys[1 - cur][:, HALF:W])
                cur = 1 - cur
                for e in range(LOGW - 2, -1, -1):
                    columns_apart(1 << e)
            assert steps == SORTED and cur == held[LOGN]

            def linked(semaphore, start=0):
                count = start

                def link(ins):
                    nonlocal count
                    count += 1
                    ins.then_inc(semaphore, 1)
                    dve.wait_ge(semaphore, count)
                return link

            link = linked(s_dec)
            dve.wait_ge(s_srt, 32)
            bits = srt[:, :].bitcast(I32)
            link(dve.tensor_scalar(seg[:, :], bits, DST_BITS, None, ALU.logical_shift_right))
            link(dve.tensor_scalar(nbr[:, :], bits[:, 1:], (1 << DST_BITS) - 1, None, ALU.bitwise_and))
            link(dve.tensor_tensor(same[:, :], seg[:, 1:], seg[:, 0:ROUNDS], ALU.is_equal))
            link(dve.tensor_copy(col[:, CONT:CONT + 1], same[:, 0:1]))
            link(dve.memset(same[:, 0:1], 0.0))
            link(dve.tensor_scalar(node_f, seg[:, 1:], float(-SEG0), None, ALU.add))
            link(dve.tensor_scalar(node_t, node_f, 1.0 / NT, -(NT - 1) / (2.0 * NT), ALU.mult, ALU.add))
            link(dve.tensor_scalar(node_t, node_t, ROUNDER, None, ALU.add))
            link(dve.tensor_scalar(node_t, node_t, -ROUNDER, None, ALU.add))
            link(dve.tensor_copy(node_p[:, :], node_t))
            link(dve.scalar_tensor_tensor(out=node_i[:, :], in0=node_t, scalar=float(-NT), in1=node_f,
                                          op0=ALU.mult, op1=ALU.add))
            link(dve.tensor_scalar(node_t, node_f, node_f[:, 0:1], 0.0, ALU.is_equal, ALU.add,
                                   accum_out=col[:, L_FIRST:L_FIRST + 1]))
            link(dve.tensor_scalar(col[:, WHOLE:WHOLE + 1], col[:, L_FIRST:L_FIRST + 1], float(ROUNDS), None, ALU.is_equal))
            link(dve.tensor_tensor(col[:, CARRY_ON:CARRY_ON + 1], col[:, WHOLE:WHOLE + 1], col[:, CONT:CONT + 1], ALU.mult))
            link(dve.tensor_tensor(first_at[:, :], col[:, L_FIRST:L_FIRST + 1], cst[:, C_ROW:C_ROW + 1], ALU.add))
            link(dve.memset(hot_p[:, 0, 0, :], 0.0))
            link(dve.memset(hot_i[:, 0, 0, :], 0.0))

            fix = linked(s_fix)
            fix(dve.tensor_scalar(w_diag[:, :], ident, col[:, CARRY_ON:CARRY_ON + 1], None, ALU.mult))
            fix(dve.memset(carry_t[:, :, 0:1], 0.0))
            dve.wait_ge(s_zt, 1)
            fix(dve.tensor_copy(w_row[:, :], wrow_ps))

            dve.wait_ge(s_wcat, 1)
            with dve.Fori(0, BODIES) as i:
                for h in range(2):
                    t0 = 2 * HR * i + HR * h
                    dve.wait_ge(s_tab[h], 16 * len(STORE_PARTS) * i + 16)
                    for g, rounds in enumerate(GATHER_GROUPS):
                        if g == 1:
                            dve.wait_ge(s_hot_free, 2 * i + h + 1)
                            dve.tensor_tensor(hot_p[:, h, :, :], iota[:, :].unsqueeze(1).to_broadcast([P, HR, P]),
                                              node_p[:, bass.ds(t0, HR)].unsqueeze(2).to_broadcast([P, HR, P]), ALU.is_equal)
                            dve.tensor_tensor(hot_i[:, h, :, :], iota[:, 0:NT].unsqueeze(1).to_broadcast([P, HR, NT]),
                                              node_i[:, bass.ds(t0, HR)].unsqueeze(2).to_broadcast([P, HR, NT]),
                                              ALU.is_equal).then_inc(s_hot, 1)
                        dve.wait_ge(s_rows[h][g], 16 * len(rounds) * i + 16 * len(rounds))
                        for r in rounds:
                            dve.wait_ge(s_acc, t0 + r + 1)
                            slot = h * HR + r
                            dve.scalar_tensor_tensor(out=runmax[:, slot, :], in0=runmax[:, slot - 1 if slot else 2 * HR - 1, :],
                                                     scalar=same_now[:, h, r:r + 1], in1=ring[:, slot, :],
                                                     op0=ALU.mult, op1=ALU.max).then_inc(s_acc, 1)

            dve.wait_ge(s_zt, 2)
            for c in range(DC):
                fix(dve.tensor_tensor_scan(carry_t[:, c, 1:P + 1], w_row[:, :], z_ps[:, c * P:(c + 1) * P], 0.0, ALU.mult, ALU.max))

            link = linked(s_cnt)
            dve.wait_ge(s_hot_free, 2 + 2 * BODIES)
            link(dve.tensor_copy(cnt, cnt_ps))
            link(dve.tensor_tensor_scan(incl, ones[:, 0:NT], cnt, 0.0, ALU.mult, ALU.add))
            dve.wait_ge(s_off, 1)
            link(dve.tensor_copy(col[:, OFF:OFF + 1], off_ps))
            link(dve.tensor_scalar(last, incl, col[:, OFF:OFF + 1], -1.0, ALU.add, ALU.add))
            link(dve.tensor_tensor(first, last, cnt, ALU.subtract))
            middle = (ROUNDS - 1) / 2.0
            link(dve.tensor_scalar(e_p, last, 1.0 / ROUNDS, -middle / ROUNDS, ALU.mult, ALU.add))
            link(dve.tensor_scalar(e_p, e_p, ROUNDER, None, ALU.add))
            link(dve.tensor_scalar(e_p, e_p, -ROUNDER, None, ALU.add))
            link(dve.tensor_scalar(s_p, first, 1.0 / ROUNDS, (1 - middle) / ROUNDS, ALU.mult, ALU.add))
            link(dve.tensor_scalar(s_p, s_p, ROUNDER, None, ALU.add))
            link(dve.tensor_scalar(s_p, s_p, -ROUNDER, None, ALU.add))
            link(dve.tensor_tensor(t_a, e_p, s_p, ALU.not_equal))
            link(dve.tensor_tensor(t_b, e_p, last, ALU.subtract))
            link(dve.scalar_tensor_tensor(out=t_b, in0=t_b, scalar=float(FIX0), in1=t_a, op0=ALU.add, op1=ALU.mult))
            link(dve.tensor_tensor(last, last, t_b, ALU.add))
            link(dve.tensor_scalar(t_a, cnt, 0.0, None, ALU.is_equal))
            link(dve.tensor_scalar(t_b, last, -1.0, float(ZERO_ROW), ALU.mult, ALU.add))
            link(dve.tensor_tensor(t_b, t_b, t_a, ALU.mult))
            link(dve.tensor_tensor(node_at[:, :], last, t_b, ALU.add))

            dve.wait_ge(s_zt, 3)
            dve.wait_ge(s_first, 16)
            dve.scalar_tensor_tensor(out=fix_rows, in0=carry_ps, scalar=col[:, CONT:CONT + 1], in1=first_rows,
                                     op0=ALU.mult, op1=ALU.max).then_inc(s_fix, 1)

            def scales(g, s):
                cols = bass.ds(g * HG, HG)
                dve.wait_ge(s_std, g + 1)
                dve.reciprocal(rstd[0:NP, cols], std[0:NP, cols]).then_inc(s_rstd, 1)
                dve.wait_ge(s_rstd, g + 1)
                dve.scalar_tensor_tensor(out=shift[0:NP, cols], in0=mv[0:NP, s, :, 0], scalar=-1.0,
                                         in1=rstd[0:NP, cols], op0=ALU.mult, op1=ALU.mult).then_inc(s_scale, 1)

            def tail_group(g, s, warm):
                def add(j):
                    n = g * HG + j
                    dve.wait_ge(s_y, n + 1)
                    y = base[0:NP, bass.ds(n * D, D)]
                    dve.tensor_tensor(y, mm_ps[0:NP, (s * HG + j) % 2, 0:D], y, ALU.add).then_inc(s_sum, 1)

                def statistics(j):
                    n = g * HG + j
                    dve.wait_ge(s_sum, n + 3)
                    dve.sem_inc(s_seen, 1)
                    dve.bn_stats(stats[0:NP, s, j, :], base[0:NP, bass.ds(n * D, D)]).then_inc(s_stat, 1)

                add(0)
                for j in range(HG):
                    if j + 1 < HG:
                        add(j + 1)
                    statistics(j)
                    if warm and j == 3:
                        scales(g - 1, 1 - s)
                dve.wait_ge(s_stat, g * HG + HG)
                dve.sem_inc(s_seen, 1)
                for j in range(HG):
                    ins = dve.bn_aggr(mv[0:NP, s, j, :], stats[0:NP, s, j, :])
                ins.then_inc(s_var, 1)

            tail_group(0, 0, False)
            tail_group(1, 1, True)
            with dve.Fori(1, GROUPS // 2) as b:
                tail_group(2 * b, 0, True)
                tail_group(2 * b + 1, 1, True)
            scales(GROUPS - 1, 1)
            dve.wait_ge(s_scale, GROUPS)
            for n in range(NT - HG, NT):
                y = base[0:NP, n * D:(n + 1) * D]
                dve.tensor_scalar(y, y, rstd[0:NP, n:n + 1], shift[0:NP, n:n + 1], ALU.mult, ALU.add).then_inc(s_last, 1)


def kernel(x, src, dst, L0_gnn_fc_w, L0_gnn_fc_b, L0_gnn_weights_matrix):
    import numpy as np
    import concourse.bacc as bacc
    from concourse.bass_utils import run_bass_kernel_spmd

    p = np.arange(P)
    consts = np.zeros((P, C_ALL), np.float32)
    consts[:, C_ID:C_ID + P] = np.eye(P)
    consts[:, C_TRI:C_TRI + P] = p[:, None] < p[None, :]
    consts[:, C_IOTA:C_IOTA + P] = p[None, :]
    down = [(p >> n) & 1 for n in range(8)]
    for n in range(8):
        consts[:, C_SIGN + n] = 1 - 2 * (down[n] if n == 0 else down[n] ^ down[n - 1])
    consts[:, C_ROW] = p * ROUNDS - 1
    consts[:, C_ONE:C_ONE + P] = 1

    given = {"x": x, "src": src, "dst": dst, "fc_w": L0_gnn_fc_w, "fc_b": L0_gnn_fc_b,
             "wm": L0_gnn_weights_matrix, "consts": consts}
    nc = bacc.Bacc("TRN2", target_bir_lowering=False, num_devices=1)
    arrays, args = {}, []
    for name, a in given.items():
        a = np.ascontiguousarray(a)
        arrays[f"in_{name}"] = a
        args.append(nc.dram_tensor(f"in_{name}", a.shape, mybir.dt.from_np(a.dtype), kind="ExternalInput").ap())
    out = nc.dram_tensor("out_y", (NODES, D), F32, kind="ExternalOutput").ap()
    build(nc, *args, out)
    return run_bass_kernel_spmd(nc, [arrays], core_ids=[0]).results[0]["out_y"]
```

```python
from contextlib import ExitStack

import concourse.bass as bass
from concourse import mybir

ALU = mybir.AluOpType
ACT = mybir.ActivationFunctionType
F32 = mybir.dt.float32
BF16 = mybir.dt.bfloat16
I32 = mybir.dt.int32

P = 128
D = 256
DC = D // P
NODES = 6250
NP = 125
NT = NODES // NP
SPREAD = 112
EDGES = 100000
EC = EDGES // NP

LOGW = 10
W = 1 << LOGW
LOGN = LOGW + 7
HALF = W // 2
DST_BITS = 13
MARK = 0x20000000
PAD_KEY = float(2.0 ** 127)
BELOW = P // 2 * (W - EC)
SEG0 = MARK >> DST_BITS

ROUNDS = -(-EDGES // P)
HR = 17
BODIES = ROUNDS // (2 * HR)
GROUPS_OF_ROUNDS = [range(0, 5), range(5, 10), range(10, 14), range(14, HR)]
FIX0 = P * ROUNDS
ZERO_ROW = FIX0 + P
TABLE = ZERO_ROW + 1
ROUNDER = float(3 << 22)

HG = 5
GROUPS = NT // HG
AHEAD = NT - 2 * BODIES
LOOPED = 6
PER_LEVEL = -(-(NT - LOOPED * HG) // (LOGN - LOGW))
NORM_AFTER = [[], [], [0], [1, 2], [3, 4]]
EPS = 1e-5

C_ID, C_TRI, C_IOTA, C_SIGN, C_ROW, C_ONE = 0, P, 2 * P, 3 * P, 3 * P + 8, 4 * P
C_ALL = 5 * P


def build(nc, x, src, dst, fc_w, fc_b, wm, consts, out):
    assert NP * NT == NODES and AHEAD >= 2 and NP * EC == EDGES and 2 * HR * BODIES == ROUNDS and EC <= W
    ctx = ExitStack()
    with ctx:
        def sb(name, shape, dt):
            return ctx.enter_context(nc.sbuf_tensor(name, shape, dt))

        def ps(name, shape):
            return ctx.enter_context(nc.psum_tensor(name, shape, F32))

        def sem(name):
            return ctx.enter_context(nc.semaphore(name))

        keys_dram = nc.dram_tensor("sorted_keys", [P * W], F32).ap()
        h_dram = nc.dram_tensor("h_rows", [NODES, D], F32).ap()
        table = nc.dram_tensor("running_max", [TABLE, D], F32).ap()
        table_rounds = table[0:FIX0, :].rearrange("(p c) f -> p c f", c=ROUNDS)

        base = sb("base", [P, NT * D], F32)
        cst = sb("cst", [P, C_ALL], F32)
        w_cat = sb("w_cat", [P, DC, 2 * D], F32)
        w2 = sb("w2", [P, DC, D], F32)
        bias = sb("bias", [1, D], F32)
        x_again = sb("x_again", [P, 2, D], F32)
        xt = sb("xt", [P, 2, DC, P], F32)
        ring = sb("ring", [P, 2 * HR, D], F32)
        runmax = sb("runmax", [P, 2 * HR, D], F32)
        srt = sb("srt", [P, ROUNDS + 1], F32)
        seg = sb("seg", [P, ROUNDS + 1], I32)
        nbr = sb("nbr", [P, ROUNDS], I32)
        same = sb("same", [P, ROUNDS], F32)
        node_p = sb("node_p", [P, ROUNDS], BF16)
        node_i = sb("node_i", [P, ROUNDS], BF16)
        nbr_now = sb("nbr_now", [P, 2, HR], I32)
        same_now = sb("same_now", [P, 2, HR], F32)
        iota = sb("iota", [P, P], BF16)
        hot_p = sb("hot_p", [P, 2, HR, P], BF16)
        hot_i = sb("hot_i", [P, 2, HR, NT], BF16)
        col = sb("col", [P, 16], F32)
        first_at = sb("first_at", [P, 1], I32)
        node_at = sb("node_at", [P, NT], I32)
        node_math = sb("node_math", [P, 8, NT], F32)
        stats = sb("stats", [P, 2, HG, 6], F32)
        mv = sb("mv", [P, 2, HG, 2], F32)
        std = sb("std", [P, NT], F32)
        rstd = sb("rstd", [P, NT], F32)
        shift = sb("shift", [P, NT], F32)
        eps = sb("eps", [P, 1], F32)
        w_diag = sb("w_diag", [P, P], F32)
        w_row = sb("w_row", [P, P], F32)
        carry_t = sb("carry_t", [P, DC, P + 1], F32)

        flat = ring[:, :, :].rearrange("p a b -> p (a b)")
        keys = [flat[:, 0:W], flat[:, W:2 * W]]
        signed = flat[:, 2 * W:3 * W]
        upper = flat[:, 3 * W:3 * W + HALF]
        upper_half = flat[:, 3 * W + HALF:4 * W]
        src_in = flat[:, 4 * W:4 * W + EC].bitcast(I32)
        dst_in = flat[:, 5 * W:5 * W + EC].bitcast(I32)
        key_bits = keys[1].bitcast(I32)
        flat_max = runmax[:, :, :].rearrange("p a b -> p (a b)")
        node_f = flat_max[:, 20 * D:20 * D + ROUNDS]
        node_t = flat_max[:, 24 * D:24 * D + ROUNDS]
        xg = [runmax[:, s * HG:(s + 1) * HG, :] for s in range(2)]
        hg = [runmax[:, (2 + s) * HG:(3 + s) * HG, :] for s in range(2)]
        first_rows = ring[:, 20, :]
        fix_rows = ring[:, 21, :]
        late_rows = ring[:, 22, :]
        cnt, incl, last, first, e_p, s_p, t_a, t_b = (node_math[:, n, :] for n in range(8))
        agg = [ring[:, s * HG:(s + 1) * HG, :] for s in range(2)]

        tp = ps("tp", [P, W])
        bp = ps("bp", [P, W])
        xt_ps = ps("xt_ps", [P, 2, 512])
        mm_ps = ps("mm_ps", [P, 2, 512])
        cnt_ps = tp[:, 0:NT]
        off_ps = tp[:, HALF:HALF + 1]
        z_ps = bp[:, 0:D]
        wrow_ps = bp[:, HALF:HALF + P]
        carry_ps = xt_ps[:, 0, 0:D]
        y_ps = [mm_ps[:, 0, 0:D], mm_ps[:, 1, 0:D], bp[:, 0:D], bp[:, HALF:HALF + D], tp[:, 0:D]]

        ident = cst[:, C_ID:C_ID + P]
        tri = cst[:, C_TRI:C_TRI + P]
        ones = cst[:, C_ONE:C_ONE + P]
        LATE = len(GROUPS_OF_ROUNDS[-1])
        L_FIRST, CONT, WHOLE, CARRY_ON, OFF, EARLY, ENDS_AT = range(7)

        s_src = sem("src_loaded")
        s_dst = sem("dst_loaded")
        s_consts = sem("consts_loaded")
        s_weights = sem("weights_loaded")
        s_x = [sem(f"x_loaded_{s}") for s in range(2)]
        s_wcat = sem("w_cat_ready")
        s_xt_t = sem("x_transposed")
        s_xt_c = sem("xt_copied")
        s_mm = sem("h_product_done")
        s_h = sem("h_evacuated")
        s_h_st = [sem(f"h_stored_{s}") for s in range(2)]
        s_sort = sem("sort_steps")
        s_run = [sem(f"sort_steps_half_{h}") for h in range(2)]
        s_quarter = sem("first_quarter_turns_back")
        s_signed = sem("signed_pieces")
        s_tr = sem("sort_transposes")
        s_up = sem("upper_copied")
        s_x_again = [sem(f"x_loaded_again_{s}") for s in range(2)]
        s_b_turned = sem("base_x_transposed")
        s_b_copied = sem("base_xt_copied")
        s_b_mm = sem("base_product_done")
        s_base = sem("base_ready")
        s_keys_st = sem("keys_stored")
        s_srt_start = sem("first_rounds_keys_loaded")
        s_srt = sem("sorted_loaded")
        s_dec = sem("decoded")
        s_staged = sem("halves_staged")
        s_same = sem("first_marks_staged")
        s_pool = sem("pool_halves")
        s_rows = [[sem(f"rows_{h}_{g}") for g in range(len(GROUPS_OF_ROUNDS))] for h in range(2)]
        s_acc = sem("rounds_done")
        s_tab = [sem(f"table_stored_{h}") for h in range(2)]
        s_tab_end = [sem(f"last_group_stored_{h}") for h in range(2)]
        s_hot = sem("onehots_ready")
        s_hot_free = sem("onehots_free")
        s_cnt = sem("count_steps")
        s_off = sem("offsets_ready")
        s_first = sem("first_rows_loaded")
        s_zt = sem("carry_transposes")
        s_fix = sem("fix_steps")
        s_fix_st = sem("fix_rows_stored")
        s_agg = [sem(f"agg_loaded_{j}") for j in range(2 * HG)]
        s_at = sem("agg_transposed")
        s_at_c = sem("agg_copied")
        s_y = sem("agg_product_done")
        s_sum = sem("y_summed")
        s_stat = sem("statistics_ready")
        s_seen = sem("statistics_seen")
        s_var = sem("variance_ready")
        s_std = sem("deviation_ready")
        s_rstd = sem("rstd_ready")
        s_scale = sem("scales_ready")
        s_norm = sem("tiles_normed")
        s_last = sem("last_group_normed")
        s_out = sem("out_stored")

        PARTS = (slice(0, SPREAD), slice(SPREAD, NP))
        x_tiles = x.rearrange("(p i) f -> p i f", i=NT)
        x_rows = x.rearrange("(p i) f -> p (i f)", i=NT)
        h_tiles = h_dram.rearrange("(p i) f -> p i f", i=NT)
        out_rows = out.rearrange("(p i) f -> p (i f)", i=NT)

        SETUP = 4
        PARTED = SETUP + LOGW * (LOGW - 1) // 2 + 1
        run_end = {LOGW: LOGW - 1}
        held = {LOGW: LOGW * (LOGW + 1) // 2 % 2}
        for k in range(LOGW + 1, LOGN + 1):
            run_end[k] = run_end[k - 1] + k
            held[k] = (held[k - 1] + k) % 2

        def turned_end(k):
            return run_end[k - 1] + (k - LOGW)

        def turned_held(k):
            return (held[k - 1] + k - LOGW) % 2

        def turned_back(b):
            return tp[:, HALF + (b - 2) * P:HALF + (b - 1) * P] if b in (2, 3) else bp[:, b * P:(b + 1) * P]

        def half(h):
            return slice(h * HALF, (h + 1) * HALF)

        state = runmax[:, 2 * HR - 1, :]
        zeros_p, zeros_i = hot_p[:, 0, 0, :], hot_i[:, 0, 0, :]
        CARRIED = 5 + LATE
        FIX_DONE = CARRIED + 2
        CNT_DONE = 19
        SAME_DECODED = 6
        DECODED = 19 + LATE

        block = ctx.enter_context(nc.Block())

        @block.sync
        def _(sp):
            sp.dma_start(src_in[0:NP, :], src.rearrange("(p c) -> p c", c=EC)).then_inc(s_src, 16)
            sp.dma_start(dst_in[0:NP, :], dst.rearrange("(p c) -> p c", c=EC)).then_inc(s_dst, 16)
            sp.dma_start(cst[:, :], consts).then_inc(s_consts, 16)

            def load_x(g):
                for part in PARTS:
                    sp.dma_start(xg[g % 2][part, :, :], x_tiles[part, g * HG:(g + 1) * HG, :]).then_inc(s_x[g % 2], 16)

            load_x(0)
            sp.dma_start(w_cat[:, :, 0:D], fc_w.rearrange("(c p) n -> p c n", c=DC)).then_inc(s_weights, 16)
            sp.dma_start(w_cat[:, :, D:2 * D], wm[0:D, :].rearrange("(c p) n -> p c n", c=DC)).then_inc(s_weights, 16)
            sp.dma_start(w2[:, :, :], wm[D:2 * D, :].rearrange("(c p) n -> p c n", c=DC)).then_inc(s_weights, 16)
            sp.dma_start(bias[:, :], fc_b.rearrange("(a n) -> a n", a=1)).then_inc(s_weights, 16)
            load_x(1)
            sp.wait_ge(s_acc, 1)
            for h in range(2):
                sp.dma_start(table[ZERO_ROW:ZERO_ROW + 1, h * P:(h + 1) * P], state[0:1, h * P:(h + 1) * P]).then_inc(s_tab[h], 16)
            for g in range(GROUPS):
                sp.wait_ge(s_h, 2 + HG * (g + 1))
                for part in PARTS:
                    sp.dma_start(h_tiles[part, g * HG:(g + 1) * HG, :], hg[g % 2][part, :, :]).then_inc(s_h_st[g % 2], 16)
                if g + 2 < GROUPS:
                    sp.wait_ge(s_xt_t, HG * (g + 1))
                    load_x(g + 2)

            def load_x_again(n, slot):
                sp.dma_start(x_again[0:NP, slot, :], x_rows[:, bass.ds(n * D, D)]).then_inc(s_x_again[slot], 16)

            for n in range(2):
                load_x_again(n, n)
            for h in (1, 0):
                sp.wait_ge(s_run[h], run_end[LOGN])
                sp.dma_start(keys_dram.rearrange("(p c) -> p c", c=W)[:, half(h)], keys[held[LOGN]][:, half(h)]).then_inc(s_keys_st, 16)
            sp.wait_ge(s_keys_st, 32)
            chunks = keys_dram[BELOW - 1:BELOW - 1 + P * ROUNDS].rearrange("(p c) -> p c", c=ROUNDS)
            sp.dma_start(srt[:, 0:2 * HR + 1], chunks[:, 0:2 * HR + 1]).then_inc(s_srt_start, 16)
            sp.dma_start(srt[:, 2 * HR + 1:ROUNDS], chunks[:, 2 * HR + 1:]).then_inc(s_srt, 16)
            ends = keys_dram[BELOW - 1 + ROUNDS:BELOW - 1 + ROUNDS + P * ROUNDS].rearrange("(p c) -> p c", c=ROUNDS)
            sp.dma_start(srt[:, ROUNDS:ROUNDS + 1], ends[:, 0:1], allow_slow_non_contiguous=True).then_inc(s_srt, 16)
            for n in range(2, AHEAD):
                sp.wait_ge(s_b_turned, n - 1)
                load_x_again(n, n % 2)
            with sp.Fori(0, BODIES) as i:
                for h in range(2):
                    sp.wait_ge(s_b_turned, AHEAD + 2 * i + h - 1)
                    load_x_again(AHEAD + 2 * i + h, h)
                    for rounds in GROUPS_OF_ROUNDS:
                        a, e = rounds.start, rounds.stop
                        stored = s_tab[h] if e < HR else s_tab_end[h]
                        sp.wait_ge(s_acc, 1 + 2 * HR * i + HR * h + e)
                        sp.dma_start(table_rounds[:, bass.ds(2 * HR * i + HR * h + a, e - a), :],
                                     runmax[:, h * HR + a:h * HR + e, :]).then_inc(stored, 16)
            sp.wait_ge(s_fix, FIX_DONE)
            sp.dma_start(table[FIX0:FIX0 + P, :], fix_rows).then_inc(s_fix_st, 16)

            def store(g):
                for part in PARTS:
                    sp.dma_start(out_rows[part, bass.ds(g * HG * D, HG * D)],
                                 base[part, bass.ds(g * HG * D, HG * D)]).then_inc(s_out, 16)

            with sp.Fori(0, GROUPS - 1) as g:
                sp.wait_ge(s_norm, g * HG + HG)
                store(g)
            sp.wait_ge(s_last, HG - 2)
            sp.wait_ge(s_norm, NT - HG + 2)
            store(GROUPS - 1)
            sp.wait_ge(s_out, 32 * GROUPS)
            for s in range(2):
                sp.wait_ge(s_h_st[s], 32 * (GROUPS // 2))

        @block.gpsimd
        def _(pool):
            pool.wait_ge(s_consts, 16)
            pool.wait_ge(s_weights, 64)
            for c in range(DC):
                diag = w_cat[:, c, D + c * P:D + (c + 1) * P]
                pool.tensor_tensor(diag, diag, ident, ALU.add)
            pool.tensor_copy(iota[:, :], cst[:, C_IOTA:C_IOTA + P])
            pool.memset(eps[:, :], EPS).then_inc(s_wcat, 1)
            for s in range(2):
                pool.wait_ge(s_h_st[s], 32 * (GROUPS // 2))
            with pool.Fori(0, BODIES) as i:
                for h in range(2):
                    pool.wait_ge(s_staged, 2 * i + h + 1)
                    pool.sem_inc(s_pool, 1)
                    for g, rounds in enumerate(GROUPS_OF_ROUNDS):
                        for r in rounds:
                            pool.indirect_dma_start(
                                ring[:, h * HR + r, :], None, h_dram,
                                bass.IndirectOffsetOnAxis(ap=nbr_now[:, h, r:r + 1], axis=0)).then_inc(s_rows[h][g], 16)
            for h in range(2):
                pool.wait_ge(s_tab[h], 16 + 16 * (len(GROUPS_OF_ROUNDS) - 1) * BODIES)
            pool.wait_ge(s_tab_end[0], 16 + 16 * BODIES)
            pool.indirect_dma_start(first_rows, None, table[0:FIX0, :],
                                    bass.IndirectOffsetOnAxis(ap=first_at[:, :], axis=0)).then_inc(s_first, 16)
            pool.wait_ge(s_tab_end[1], 16 + 16 * BODIES)
            pool.wait_ge(s_cnt, CNT_DONE)
            pool.wait_ge(s_fix_st, 16)
            for t in range(NT):
                if t >= 2 * HG:
                    pool.wait_ge(s_at, t - 2 * HG + 1)
                pool.indirect_dma_start(agg[t // HG % 2][:, t % HG, :], None, table,
                                        bass.IndirectOffsetOnAxis(ap=node_at[:, t:t + 1], axis=0)).then_inc(s_agg[t % (2 * HG)], 16)

        def turn_x(pe, rows, slot):
            for c in range(DC):
                ins = pe.transpose(xt_ps[:, slot, c * P:c * P + NP], rows[0:NP, c * P:(c + 1) * P], ident[0:NP, 0:NP])
            return ins

        def h_products(pe, tiles):
            def turn(g, s, j):
                slot = (s * HG + j) % 2
                if j == 0:
                    pe.wait_ge(s_x[s], 16 * (g - s) + 32)
                pe.wait_ge(s_xt_c, g * HG + j + 1)
                turn_x(pe, xg[s][:, j, :], slot).then_inc(s_xt_t, 1)

            def product(g, s, j):
                slot = (s * HG + j) % 2
                pe.wait_ge(s_xt_c, g * HG + j + 3)
                pe.wait_ge(s_h, g * HG + j + 1)
                for c in range(DC):
                    pe.matmul(mm_ps[0:NP, slot, 0:D], xt[:, slot, c, 0:NP], w_cat[:, c, 0:D], start=(c == 0), stop=False)
                pe.matmul(mm_ps[0:NP, slot, 0:D], ones[0:1, 0:NP], bias[0:1, :], start=False, stop=True).then_inc(s_mm, 1)

            turn(*tiles[0])
            for n, tile in enumerate(tiles):
                if n + 1 < len(tiles):
                    turn(*tiles[n + 1])
                product(*tile)

        def copy_turned(act, turned, copied, n, slot):
            act.wait_ge(turned, n + 1)
            act.copy(xt[:, slot, :, 0:NP],
                     xt_ps[:, slot, 0:D].rearrange("p (c n) -> p c n", c=DC)[:, :, 0:NP]).then_inc(copied, 1)

        def h_evacuate(act, tiles):
            def copy_tile(g, s, j):
                copy_turned(act, s_xt_t, s_xt_c, g * HG + j, (s * HG + j) % 2)

            copy_tile(*tiles[0])
            for n, (g, s, j) in enumerate(tiles):
                if n + 1 < len(tiles):
                    copy_tile(*tiles[n + 1])
                act.wait_ge(s_mm, g * HG + j + 1)
                if j == 0 and not (isinstance(g, int) and g < 2):
                    act.wait_ge(s_h_st[s], 16 * (g - s))
                act.activation(hg[s][0:NP, j, :], mm_ps[0:NP, (s * HG + j) % 2, 0:D], ACT.Relu).then_inc(s_h, 1)

        def group_tiles(g, s):
            return [(g, s, j) for j in range(HG)]

        def level_tiles(k):
            ahead = LOOPED * HG + PER_LEVEL * (k - LOGW - 1)
            return [(n // HG, n // HG % 2, n % HG) for n in range(ahead, min(NT, ahead + PER_LEVEL))]

        def level_base(k, per_level):
            return per_level * (k - LOGW - 1)

        def pairs(buf, d):
            v = buf.rearrange("p (a two d) -> p a two d", two=2, d=d)
            return v[:, :, 0, :], v[:, :, 1, :]

        @block.tensor
        def _(pe):
            pe.wait_ge(s_wcat, 1)
            for s in range(2):
                h_products(pe, group_tiles(s, s))
            with pe.Fori(1, LOOPED // 2) as b:
                for s in range(2):
                    h_products(pe, group_tiles(2 * b + s, s))
            for k in range(LOGW + 1, LOGN + 1):
                for n, b in enumerate((4, 5, 6, 7, 0, 1, 2, 3)):
                    if n % 2 == 0:
                        pe.wait_ge(s_signed, level_base(k, 4) + n // 2 + 1)
                    ins = pe.transpose(tp[:, b * P:(b + 1) * P], signed[:, b * P:(b + 1) * P], ident)
                    if n % 4 == 3:
                        ins.then_inc(s_tr, 1)
                for b in (4, 5, 6, 7, 0, 1, 2, 3):
                    if b == 4:
                        pe.wait_ge(s_run[1], turned_end(k))
                    if b == 0:
                        pe.wait_ge(s_quarter, k - LOGW)
                    if b == 2:
                        pe.wait_ge(s_run[0], turned_end(k))
                    ins = pe.transpose(turned_back(b), keys[turned_held(k)][:, b * P:(b + 1) * P], ident)
                    if b in (7, 1, 3):
                        ins.then_inc(s_tr, 1)
                h_products(pe, level_tiles(k))

            def turn_base(n, slot):
                pe.wait_ge(s_x_again[slot], 8 * (n - slot) + 16)
                pe.wait_ge(s_b_copied, n + 1)
                turn_x(pe, x_again[:, slot, :], slot).then_inc(s_b_turned, 1)

            def product_base(n, slot):
                pe.wait_ge(s_b_copied, n + 3)
                pe.wait_ge(s_base, n + 1)
                for c in range(DC):
                    ins = pe.matmul(mm_ps[0:NP, slot, 0:D], xt[:, slot, c, 0:NP], w_cat[:, c, D:2 * D],
                                    start=(c == 0), stop=(c == DC - 1))
                ins.then_inc(s_b_mm, 1)

            pe.wait_ge(s_h, 2 + NT)
            for n in range(AHEAD):
                turn_base(n, n % 2)
                product_base(n, n % 2)

            pe.wait_ge(s_fix, 1)
            pe.matmul(wrow_ps, ones, w_diag[:, :], start=True, stop=True).then_inc(s_zt, 1)

            pe.wait_ge(s_dec, DECODED)
            pe.matmul(cnt_ps, zeros_p, zeros_i, start=True, stop=False, skip_group_check=True).then_inc(s_hot_free, 2)
            def count(i, h):
                pe.wait_ge(s_hot, 2 * i + h + 1)
                for r in range(HR):
                    ins = pe.matmul(cnt_ps, hot_p[:, h, r, :], hot_i[:, h, r, :], start=False, stop=False,
                                    skip_group_check=True)
                ins.then_inc(s_hot_free, 1)

            with pe.Fori(0, BODIES - 1) as i:
                for h in range(2):
                    count(i, h)
                    turn_base(AHEAD + 2 * i + h, h)
                    product_base(AHEAD + 2 * i + h, h)
            for h in range(2):
                count(BODIES - 1, h)
            pe.wait_ge(s_cnt, 2)
            pe.matmul(off_ps, tri, incl[:, NT - 1:NT], start=True, stop=True).then_inc(s_off, 1)
            for h in range(2):
                turn_base(NT - 2 + h, h)
                product_base(NT - 2 + h, h)
            pe.wait_ge(s_acc, 1 + ROUNDS)
            for c in range(DC):
                ins = pe.transpose(z_ps[:, c * P:(c + 1) * P], state[:, c * P:(c + 1) * P], ident)
            ins.then_inc(s_zt, 1)
            pe.wait_ge(s_fix, CARRIED)
            for c in range(DC):
                ins = pe.transpose(carry_ps[:, c * P:(c + 1) * P], carry_t[:, c, 0:P], ident)
            ins.then_inc(s_zt, 1)

            def turn(g, s, j):
                slot = (s * HG + j) % 2
                pe.wait_ge(s_agg[s * HG + j], 8 * (g - s) + 16)
                pe.wait_ge(s_at_c, g * HG + j + 1)
                for c in range(DC):
                    ins = pe.transpose(xt_ps[:, slot, c * P:(c + 1) * P], agg[s][:, j, c * P:(c + 1) * P], ident)
                ins.then_inc(s_at, 1)

            def product(g, s, j):
                slot = (s * HG + j) % 2
                pe.wait_ge(s_at_c, g * HG + j + 3)
                pe.wait_ge(s_sum, g * HG + j + 1)
                for c in range(DC):
                    ins = pe.matmul(y_ps[j][0:NP, :], xt[:, slot, c, 0:NP], w2[:, c, :],
                                    start=(c == 0), stop=(c == DC - 1))
                ins.then_inc(s_y, 1)

            pe.wait_ge(s_fix, FIX_DONE)
            turn(0, 0, 0)

            def tail_group(g, s, more=True):
                for j in range(HG):
                    if j + 1 < HG:
                        turn(g, s, j + 1)
                    elif more:
                        turn(g + 1, 1 - s, 0)
                    product(g, s, j)

            with pe.Fori(0, GROUPS // 2 - 1) as b:
                for s in range(2):
                    tail_group(2 * b + s, s)
            tail_group(GROUPS - 2, 0)
            tail_group(GROUPS - 1, 1, more=False)

        @block.scalar
        def _(act):
            act.sem_inc(s_xt_c, 2)
            act.sem_inc(s_h, 2)
            act.sem_inc(s_b_copied, 2)
            act.sem_inc(s_base, 2)
            act.sem_inc(s_at_c, 2)
            for s in range(2):
                h_evacuate(act, group_tiles(s, s))
            with act.Fori(1, LOOPED // 2) as b:
                for s in range(2):
                    h_evacuate(act, group_tiles(2 * b + s, s))
            for k in range(LOGW + 1, LOGN + 1):
                for n, h in enumerate((1, 0)):
                    act.wait_ge(s_run[h], run_end[k - 1])
                    for q in (2 * h, 2 * h + 1):
                        cols = slice(q * W // 4, (q + 1) * W // 4)
                        act.mul(signed[:, cols], keys[held[k - 1]][:, cols],
                                cst[:, C_SIGN + k - LOGW:C_SIGN + k - LOGW + 1]).then_inc(s_signed, 1)
                    act.wait_ge(s_tr, level_base(k, 5) + n + 1)
                    act.copy(upper[:, h * HALF // 2:(h + 1) * HALF // 2].rearrange("p (a d) -> p a d", d=1 << (k - LOGW - 1)),
                             pairs(tp[:, half(h)], 1 << (k - LOGW - 1))[1]).then_inc(s_up, 1)
                act.wait_ge(s_tr, level_base(k, 5) + 3)
                act.copy(upper_half, bp[:, half(1)]).then_inc(s_up, 1)
                h_evacuate(act, level_tiles(k))

            def stage_neighbours(h, t):
                return act.copy(nbr_now[:, h, :], nbr[:, bass.ds(t, HR)])

            def stage_same(h, t):
                return act.copy(same_now[:, h, :], same[:, bass.ds(t, HR)])

            def base_tile(n, slot):
                copy_turned(act, s_b_turned, s_b_copied, n, slot)
                act.wait_ge(s_b_mm, n + 1)
                act.copy(base[0:NP, bass.ds(n * D, D)], mm_ps[0:NP, slot, 0:D]).then_inc(s_base, 1)

            for n in range(2):
                base_tile(n, n)
            act.wait_ge(s_dec, 1)
            for h in range(2):
                stage_neighbours(h, h * HR).then_inc(s_staged, 1)
            for n in range(2, AHEAD):
                base_tile(n, n % 2)
            act.wait_ge(s_dec, SAME_DECODED)
            for h in range(2):
                stage_same(h, h * HR).then_inc(s_same, 1)
            with act.Fori(0, BODIES - 1) as i:
                for h in range(2):
                    base_tile(AHEAD + 2 * i + h, h)
                    act.wait_ge(s_acc, 1 + 2 * HR * i + (h + 1) * HR)
                    stage_neighbours(h, 2 * HR * (i + 1) + h * HR)
                    stage_same(h, 2 * HR * (i + 1) + h * HR).then_inc(s_staged, 1)

            for h in range(2):
                base_tile(NT - 2 + h, h)

            def deviation(g, s):
                act.wait_ge(s_var, g + 1)
                act.activation(std[0:NP, bass.ds(g * HG, HG)], mv[0:NP, s, :, 1], ACT.Sqrt,
                               bias=eps[0:NP, :]).then_inc(s_std, 1)

            def normalise(n, scaled=None):
                if scaled is not None:
                    act.wait_ge(s_scale, scaled)
                y = base[0:NP, bass.ds(n * D, D)]
                act.activation(y, y, ACT.Identity, bias=shift[0:NP, bass.ds(n, 1)],
                               scale=rstd[0:NP, bass.ds(n, 1)]).then_inc(s_norm, 1)

            def tail_group(g, s, warm):
                for j in range(HG):
                    copy_turned(act, s_at, s_at_c, g * HG + j, (s * HG + j) % 2)
                    if j == 3 and warm > 0:
                        deviation(g - 1, 1 - s)
                    if warm > 1:
                        for r in NORM_AFTER[j]:
                            normalise((g - 2) * HG + r, g - 1 if r == 0 else None)

            tail_group(0, 0, 0)
            tail_group(1, 1, 1)
            with act.Fori(1, GROUPS // 2) as b:
                tail_group(2 * b, 0, 2)
                tail_group(2 * b + 1, 1, 2)
            for n in range(NT - 2 * HG, NT - HG):
                if n == NT - HG - 1:
                    deviation(GROUPS - 1, 1)
                normalise(n, GROUPS - 1 if n == NT - 2 * HG else None)
            normalise(NT - 2, GROUPS)
            normalise(NT - 1)

        @block.vector
        def _(dve):
            dve.sem_inc(s_sum, HG)
            for h in range(2):
                dve.sem_inc(s_tab_end[h], 16)
            dve.memset(state, 0.0).then_inc(s_acc, 1)

            dve.memset(keys[1], PAD_KEY)
            dve.memset(keys[0][:, EC:W], PAD_KEY).then_inc(s_sort, 1)
            dve.wait_ge(s_sort, 1)
            dve.wait_ge(s_src, 16)
            dve.tensor_scalar(key_bits[0:NP, 0:EC], src_in[0:NP, :], DST_BITS, MARK, ALU.logical_shift_left,
                              ALU.bitwise_or).then_inc(s_sort, 1)
            dve.wait_ge(s_sort, 2)
            dve.wait_ge(s_dst, 16)
            dve.tensor_tensor(key_bits[0:NP, 0:EC], key_bits[0:NP, 0:EC], dst_in[0:NP, :], ALU.bitwise_or).then_inc(s_sort, 1)
            dve.wait_ge(s_sort, 3)
            dve.wait_ge(s_consts, 16)
            dve.tensor_scalar(keys[0][:, 0:EC], keys[1][:, 0:EC], cst[:, C_SIGN:C_SIGN + 1], None, ALU.mult).then_inc(s_sort, 1)

            def exchange(low, high, out_low, out_high):
                dve.tensor_tensor(out_low, low, high, ALU.min)
                return dve.tensor_tensor(out_high, low, high, ALU.max)

            def used(d):
                return -(-EC // (2 * d)) * 2 * d

            steps = SETUP
            cur = 0
            for k in range(1, LOGW + 1):
                d = 1 << (k - 1)
                dve.wait_ge(s_sort, steps)
                low, high = pairs(keys[cur][:, 0:used(d)], d)
                out_low, out_high = pairs(keys[1 - cur][:, 0:used(d)], d)
                exchange(low, high[:, :, ::-1], out_low, out_high[:, :, ::-1]).then_inc(s_sort, 1)
                cur = 1 - cur
                steps += 1
                if k < LOGW:
                    for e in range(k - 2, -1, -1):
                        dve.wait_ge(s_sort, steps)
                        cols = slice(0, used(1 << e))
                        exchange(*pairs(keys[cur][:, cols], 1 << e), *pairs(keys[1 - cur][:, cols], 1 << e)).then_inc(s_sort, 1)
                        cur = 1 - cur
                        steps += 1
            assert steps == PARTED

            def half_step(k, h, n):
                done = run_end[k] - (LOGW - 1) + n
                now = (held[k] + LOGW - 1 + n) % 2
                if done > 0:
                    dve.wait_ge(s_run[h], done)
                else:
                    dve.wait_ge(s_sort, PARTED)
                if n < LOGW - 1:
                    d = HALF >> (n + 1)
                    cols = slice(h * HALF, min((h + 1) * HALF, used(d)) if k == LOGW else (h + 1) * HALF)
                else:
                    d = 1 << (k - 1 - n)
                    cols = half(h)
                if n == LOGW - 1:
                    dve.wait_ge(s_up, level_base(k + 1, 3) + 2 - h)
                    low = pairs(tp[:, cols], d)[0]
                    high = upper[:, h * HALF // 2:(h + 1) * HALF // 2].rearrange("p (a d) -> p a d", d=d)
                else:
                    low, high = pairs(keys[now][:, cols], d)
                out_low, out_high = pairs(keys[1 - now][:, cols], d)
                if h == 0 and n == k - 1:
                    a = HALF // (4 * d)
                    exchange(low[:, 0:a], high[:, 0:a], out_low[:, 0:a], out_high[:, 0:a]).then_inc(s_quarter, 1)
                    low, high, out_low, out_high = low[:, a:], high[:, a:], out_low[:, a:], out_high[:, a:]
                exchange(low, high, out_low, out_high).then_inc(s_run[h], 1)

            def step_runs(n_steps):
                if n_steps == LOGW - 1:
                    return [range(n, n + 1) for n in range(n_steps)]
                starts = list(range(LOGW - 3)) + [LOGW - 1]
                if n_steps > LOGW + 2:
                    starts += [LOGW + 2] + list(range(LOGW + 3, n_steps - 1))
                return [range(a, e) for a, e in zip(starts, starts[1:] + [n_steps])]

            for k in range(LOGW, LOGN + 1):
                if k > LOGW:
                    dve.wait_ge(s_up, level_base(k, 3) + 3)
                    out = keys[1 - turned_held(k)]
                    for q, turned in enumerate((bp[:, 0:HALF // 2], tp[:, HALF:HALF + HALF // 2])):
                        dve.wait_ge(s_tr, level_base(k, 5) + 4 + q)
                        a, e = q * HALF // 2, (q + 1) * HALF // 2
                        high = dve.tensor_tensor(out[:, HALF + a:HALF + e], turned, upper_half[:, a:e], ALU.max)
                        low = dve.tensor_tensor(out[:, a:e], turned, upper_half[:, a:e], ALU.min)
                    high.then_inc(s_run[1], 1)
                    low.then_inc(s_run[0], 1)
                n_steps = k if k < LOGN else LOGW - 1
                for run in step_runs(n_steps):
                    for h in (1, 0):
                        for n in run:
                            half_step(k, h, n)

            def linked(semaphore, start=0):
                count = start

                def link(ins):
                    nonlocal count
                    count += 1
                    ins.then_inc(semaphore, 1)
                    dve.wait_ge(semaphore, count)
                return link

            link = linked(s_dec)
            bits = srt[:, :].bitcast(I32)
            dve.wait_ge(s_srt_start, 16)
            link(dve.tensor_scalar(nbr[:, 0:2 * HR], bits[:, 1:2 * HR + 1], (1 << DST_BITS) - 1, None, ALU.bitwise_and))
            dve.wait_ge(s_srt, 32)
            link(dve.tensor_scalar(seg[:, :], bits, DST_BITS, None, ALU.logical_shift_right))
            link(dve.tensor_scalar(nbr[:, 2 * HR:], bits[:, 2 * HR + 1:], (1 << DST_BITS) - 1, None, ALU.bitwise_and))
            link(dve.tensor_tensor(same[:, :], seg[:, 1:], seg[:, 0:ROUNDS], ALU.is_equal))
            link(dve.tensor_copy(col[:, CONT:CONT + 1], same[:, 0:1]))
            link(dve.memset(same[:, 0:1], 0.0))
            link(dve.tensor_scalar(node_f, seg[:, 1:], float(-SEG0), None, ALU.add))
            link(dve.tensor_scalar(node_t, node_f, 1.0 / NT, -(NT - 1) / (2.0 * NT), ALU.mult, ALU.add))
            link(dve.tensor_scalar(node_t, node_t, ROUNDER, None, ALU.add))
            link(dve.tensor_scalar(node_t, node_t, -ROUNDER, None, ALU.add))
            link(dve.tensor_copy(node_p[:, :], node_t))
            link(dve.scalar_tensor_tensor(out=node_i[:, :], in0=node_t, scalar=float(-NT), in1=node_f,
                                          op0=ALU.mult, op1=ALU.add))
            link(dve.tensor_scalar(node_t, node_f, node_f[:, 0:1], 0.0, ALU.is_equal, ALU.add,
                                   accum_out=col[:, L_FIRST:L_FIRST + 1]))
            link(dve.tensor_scalar(col[:, WHOLE:WHOLE + 1], col[:, L_FIRST:L_FIRST + 1], float(ROUNDS), None, ALU.is_equal))
            link(dve.tensor_tensor(col[:, CARRY_ON:CARRY_ON + 1], col[:, WHOLE:WHOLE + 1], col[:, CONT:CONT + 1], ALU.mult))
            link(dve.tensor_scalar(col[:, EARLY:EARLY + 1], col[:, L_FIRST:L_FIRST + 1], float(ROUNDS - LATE), None, ALU.min))
            link(dve.tensor_tensor(first_at[:, :], col[:, EARLY:EARLY + 1], cst[:, C_ROW:C_ROW + 1], ALU.add))
            for n in range(LATE):
                link(dve.tensor_scalar(col[:, ENDS_AT + n:ENDS_AT + n + 1], col[:, L_FIRST:L_FIRST + 1],
                                       float(ROUNDS - LATE + n + 1), None, ALU.is_equal))
            link(dve.memset(hot_p[:, 0, 0, :], 0.0))
            link(dve.memset(hot_i[:, 0, 0, :], 0.0))

            fix = linked(s_fix)
            fix(dve.tensor_scalar(w_diag[:, :], ident, col[:, CARRY_ON:CARRY_ON + 1], None, ALU.mult))
            fix(dve.memset(carry_t[:, :, 0:1], 0.0))
            dve.wait_ge(s_zt, 1)
            fix(dve.tensor_copy(w_row[:, :], wrow_ps))

            def node_rows():
                link = linked(s_cnt)
                dve.wait_ge(s_hot_free, 2 + 2 * BODIES)
                link(dve.tensor_copy(cnt, cnt_ps))
                link(dve.tensor_tensor_scan(incl, ones[:, 0:NT], cnt, 0.0, ALU.mult, ALU.add))
                dve.wait_ge(s_off, 1)
                link(dve.tensor_copy(col[:, OFF:OFF + 1], off_ps))
                link(dve.tensor_scalar(last, incl, col[:, OFF:OFF + 1], -1.0, ALU.add, ALU.add))
                link(dve.tensor_tensor(first, last, cnt, ALU.subtract))
                middle = (ROUNDS - 1) / 2.0
                link(dve.tensor_scalar(e_p, last, 1.0 / ROUNDS, -middle / ROUNDS, ALU.mult, ALU.add))
                link(dve.tensor_scalar(e_p, e_p, ROUNDER, None, ALU.add))
                link(dve.tensor_scalar(e_p, e_p, -ROUNDER, None, ALU.add))
                link(dve.tensor_scalar(s_p, first, 1.0 / ROUNDS, (1 - middle) / ROUNDS, ALU.mult, ALU.add))
                link(dve.tensor_scalar(s_p, s_p, ROUNDER, None, ALU.add))
                link(dve.tensor_scalar(s_p, s_p, -ROUNDER, None, ALU.add))
                link(dve.tensor_tensor(t_a, e_p, s_p, ALU.not_equal))
                link(dve.tensor_tensor(t_b, e_p, last, ALU.subtract))
                link(dve.scalar_tensor_tensor(out=t_b, in0=t_b, scalar=float(FIX0), in1=t_a, op0=ALU.add, op1=ALU.mult))
                link(dve.tensor_tensor(last, last, t_b, ALU.add))
                link(dve.tensor_scalar(t_a, cnt, 0.0, None, ALU.is_equal))
                link(dve.tensor_scalar(t_b, last, -1.0, float(ZERO_ROW), ALU.mult, ALU.add))
                link(dve.tensor_tensor(t_b, t_b, t_a, ALU.mult))
                link(dve.tensor_tensor(node_at[:, :], last, t_b, ALU.add))

            dve.wait_ge(s_wcat, 1)
            dve.wait_ge(s_same, 2)
            def one_hots(i, h):
                t0 = 2 * HR * i + HR * h
                dve.wait_ge(s_hot_free, 2 * i + h + 1)
                dve.tensor_tensor(hot_p[:, h, :, :], iota[:, :].unsqueeze(1).to_broadcast([P, HR, P]),
                                  node_p[:, bass.ds(t0, HR)].unsqueeze(2).to_broadcast([P, HR, P]), ALU.is_equal)
                dve.tensor_tensor(hot_i[:, h, :, :], iota[:, 0:NT].unsqueeze(1).to_broadcast([P, HR, NT]),
                                  node_i[:, bass.ds(t0, HR)].unsqueeze(2).to_broadcast([P, HR, NT]),
                                  ALU.is_equal).then_inc(s_hot, 1)

            def half_of_rounds(i, h, last=False):
                t0 = 2 * HR * i + HR * h
                dve.wait_ge(s_tab[h], 16 * (len(GROUPS_OF_ROUNDS) - 1) * i + 16)
                dve.wait_ge(s_tab_end[h], 16 * i + 16)
                for g, rounds in enumerate(GROUPS_OF_ROUNDS):
                    if g == 0:
                        if last and h == 1:
                            node_rows()
                        else:
                            one_hots(i, h)
                            if last:
                                one_hots(i, 1)
                    dve.wait_ge(s_rows[h][g], 16 * len(rounds) * i + 16 * len(rounds))
                    for r in rounds:
                        dve.wait_ge(s_acc, t0 + r + 1)
                        slot = h * HR + r
                        dve.scalar_tensor_tensor(out=runmax[:, slot, :], in0=runmax[:, slot - 1 if slot else 2 * HR - 1, :],
                                                 scalar=same_now[:, h, r:r + 1], in1=ring[:, slot, :],
                                                 op0=ALU.mult, op1=ALU.max).then_inc(s_acc, 1)

            with dve.Fori(0, BODIES - 1) as i:
                for h in range(2):
                    half_of_rounds(i, h)
            for h in range(2):
                half_of_rounds(BODIES - 1, h, last=True)

            for n in range(LATE):
                rows = runmax[:, 2 * HR - LATE + n, :]
                ends_here = col[:, ENDS_AT + n:ENDS_AT + n + 1]
                if n == 0:
                    fix(dve.tensor_scalar(late_rows, rows, ends_here, None, ALU.mult))
                else:
                    fix(dve.scalar_tensor_tensor(out=late_rows, in0=rows, scalar=ends_here, in1=late_rows,
                                                 op0=ALU.mult, op1=ALU.max))
            dve.wait_ge(s_zt, 2)
            for c in range(DC):
                fix(dve.tensor_tensor_scan(carry_t[:, c, 1:P + 1], w_row[:, :], z_ps[:, c * P:(c + 1) * P], 0.0, ALU.mult, ALU.max))

            dve.wait_ge(s_zt, 3)
            fix(dve.scalar_tensor_tensor(out=late_rows, in0=carry_ps, scalar=col[:, CONT:CONT + 1], in1=late_rows,
                                         op0=ALU.mult, op1=ALU.max))
            dve.wait_ge(s_first, 16)
            dve.tensor_tensor(fix_rows, late_rows, first_rows, ALU.max).then_inc(s_fix, 1)

            def scales(g, s):
                cols = bass.ds(g * HG, HG)
                dve.wait_ge(s_std, g + 1)
                dve.reciprocal(rstd[0:NP, cols], std[0:NP, cols]).then_inc(s_rstd, 1)
                dve.wait_ge(s_rstd, g + 1)
                dve.scalar_tensor_tensor(out=shift[0:NP, cols], in0=mv[0:NP, s, :, 0], scalar=-1.0,
                                         in1=rstd[0:NP, cols], op0=ALU.mult, op1=ALU.mult).then_inc(s_scale, 1)

            def tail_group(g, s, scales_at=3):
                def add(j):
                    n = g * HG + j
                    dve.wait_ge(s_y, n + 1)
                    y = base[0:NP, bass.ds(n * D, D)]
                    dve.tensor_tensor(y, y_ps[j][0:NP, :], y, ALU.add).then_inc(s_sum, 1)

                def statistics(j):
                    n = g * HG + j
                    dve.wait_ge(s_sum, n + HG + 1)
                    dve.sem_inc(s_seen, 1)
                    dve.bn_stats(stats[0:NP, s, j, :], base[0:NP, bass.ds(n * D, D)]).then_inc(s_stat, 1)

                if isinstance(g, int) and g == 0:
                    dve.wait_ge(s_base, 2 + NT)
                add(0)
                for j in range(HG):
                    if j + 1 < HG:
                        add(j + 1)
                    statistics(j)
                    if j == scales_at:
                        scales(g - 1, 1 - s)
                dve.wait_ge(s_stat, g * HG + HG)
                dve.sem_inc(s_seen, 1)
                for j in range(HG):
                    ins = dve.bn_aggr(mv[0:NP, s, j, :], stats[0:NP, s, j, :])
                ins.then_inc(s_var, 1)

            tail_group(0, 0, scales_at=None)
            tail_group(1, 1)
            with dve.Fori(1, GROUPS // 2 - 1) as b:
                tail_group(2 * b, 0)
                tail_group(2 * b + 1, 1)
            tail_group(GROUPS - 2, 0)
            tail_group(GROUPS - 1, 1, scales_at=1)
            scales(GROUPS - 1, 1)
            dve.wait_ge(s_scale, GROUPS)
            for n in range(NT - HG, NT - 2):
                y = base[0:NP, n * D:(n + 1) * D]
                dve.tensor_scalar(y, y, rstd[0:NP, n:n + 1], shift[0:NP, n:n + 1], ALU.mult, ALU.add).then_inc(s_last, 1)


def kernel(x, src, dst, L0_gnn_fc_w, L0_gnn_fc_b, L0_gnn_weights_matrix):
    import numpy as np
    import concourse.bacc as bacc
    from concourse.bass_utils import run_bass_kernel_spmd

    p = np.arange(P)
    consts = np.zeros((P, C_ALL), np.float32)
    consts[:, C_ID:C_ID + P] = np.eye(P)
    consts[:, C_TRI:C_TRI + P] = p[:, None] < p[None, :]
    consts[:, C_IOTA:C_IOTA + P] = p[None, :]
    down = [(p >> n) & 1 for n in range(8)]
    for n in range(8):
        consts[:, C_SIGN + n] = 1 - 2 * (down[n] if n == 0 else down[n] ^ down[n - 1])
    consts[:, C_ROW] = p * ROUNDS - 1
    consts[:, C_ONE:C_ONE + P] = 1

    given = {"x": x, "src": src, "dst": dst, "fc_w": L0_gnn_fc_w, "fc_b": L0_gnn_fc_b,
             "wm": L0_gnn_weights_matrix, "consts": consts}
    nc = bacc.Bacc("TRN2", target_bir_lowering=False, num_devices=1)
    arrays, args = {}, []
    for name, a in given.items():
        a = np.ascontiguousarray(a)
        arrays[f"in_{name}"] = a
        args.append(nc.dram_tensor(f"in_{name}", a.shape, mybir.dt.from_np(a.dtype), kind="ExternalInput").ap())
    out = nc.dram_tensor("out_y", (NODES, D), F32, kind="ExternalOutput").ap()
    build(nc, *args, out)
    return run_bass_kernel_spmd(nc, [arrays], core_ids=[0]).results[0]["out_y"]
```
